# Optimizing a Trainium2 kernel written in Bass

```python
import numpy as np
import jax
import jax.numpy as jnp

def _softmax(x, axis=-1):
    return jax.nn.softmax(x, axis=axis)

def _gelu(x):
    return jax.nn.gelu(x, approximate=True)

def _silu(x):
    return jax.nn.silu(x)

def _sigmoid(x):
    return jax.nn.sigmoid(x)

def _layernorm(x, axis=-1, eps=1e-05):
    m = jnp.mean(x, axis=axis, keepdims=True)
    v = jnp.var(x, axis=axis, keepdims=True)
    return (x - m) / jnp.sqrt(v + eps)

def _scatter_add(tgt, idx, src, axis=0):
    return tgt.at[idx].add(src)

def _segment_sum(src, seg, n):
    return jax.ops.segment_sum(src, seg, n)
kernel_name = 'mk_seq_postln_d1_jaxref_r4_a609ce'

def setup_inputs(seed: int=0):
    np.random.seed(seed)
    _w = jnp.asarray

    def _L0_attn_setup():
        import jax, jax.numpy as jnp
        import numpy as np
        EMB = 512
        HEADS = 16
        HEAD_DIM = EMB // HEADS
        MIN_WINDOW = 64
        MAX_WINDOW = 64
        ROPE_BASE = 10000.0

        def _rotate_half(t):
            x1 = t[..., ::2]
            x2 = t[..., 1::2]
            return jnp.stack((-x2, x1), axis=-1).reshape(t.shape)

        def _rope_tables(seq_len, dtype):
            inv_freq = 1.0 / ROPE_BASE ** (jnp.arange(0, HEAD_DIM, 2, dtype=jnp.float32) / HEAD_DIM)
            pos = jnp.arange(seq_len, dtype=jnp.float32)
            freqs = jnp.outer(pos, inv_freq)
            emb = jnp.concatenate([freqs, freqs], axis=-1)
            return (jnp.cos(emb)[None, None].astype(dtype), jnp.sin(emb)[None, None].astype(dtype))

        def _forward(x, w_qkv, w_out, w_c1, w_c2):
            B, S, _ = x.shape
            scale = HEAD_DIM ** (-0.5)
            qkv = x @ w_qkv.T
            qkv = qkv.reshape(B, S, 3, HEADS, HEAD_DIM).transpose(2, 0, 3, 1, 4)
            q, k, v = (qkv[0], qkv[1], qkv[2])
            cos, sin = _rope_tables(S, x.dtype)
            q = q * cos + _rotate_half(q) * sin
            k = k * cos + _rotate_half(k) * sin
            scores = jnp.einsum('bhqd,bhkd->bhqk', q, k) * scale
            var = jnp.var(x.reshape(B, -1), axis=1, ddof=1)
            var_norm = jax.nn.sigmoid(var * 10.0 - 5.0)
            x_mean = x.mean(axis=1)
            hidden = jax.nn.silu(x_mean @ w_c1.T)
            learned = jax.nn.sigmoid(hidden @ w_c2.T)[:, 0]
            complexity = (var_norm + learned) / 2.0
            window_f = MIN_WINDOW + complexity * (MAX_WINDOW - MIN_WINDOW)
            window = window_f.mean().astype(jnp.int32)
            window = jnp.maximum(jnp.minimum(window, S), MIN_WINDOW)
            pos = jnp.arange(S)
            rel = pos[:, None] - pos[None, :]
            keep = (rel >= 0) & (rel < window)
            scores = jnp.where(keep[None, None], scores, -jnp.inf)
            attn = jax.nn.softmax(scores, axis=-1)
            out = jnp.einsum('bhqk,bhkd->bhqd', attn, v)
            out = out.transpose(0, 2, 1, 3).reshape(B, S, EMB)
            return out @ w_out.T
        key = jax.random.key(seed)
        ks = jax.random.split(key, 5)
        B, S = (2, 512)
        x = jax.random.normal(ks[0], (B, S, EMB), dtype=jnp.float32)
        w_qkv = jax.random.normal(ks[1], (3 * EMB, EMB), dtype=jnp.float32) * EMB ** (-0.5)
        w_out = jax.random.normal(ks[2], (EMB, EMB), dtype=jnp.float32) * EMB ** (-0.5)
        w_c1 = jax.random.normal(ks[3], (EMB // 4, EMB), dtype=jnp.float32) * 0.1 * EMB ** (-0.5)
        w_c2 = jax.random.normal(ks[4], (1, EMB // 4), dtype=jnp.float32) * 0.1 * (EMB // 4) ** (-0.5)
        return {'x': x, 'w_qkv': w_qkv, 'w_out': w_out, 'w_c1': w_c1, 'w_c2': w_c2}
    _L0_attn_in = _L0_attn_setup()

    def _L0_ffn_setup():
        import jax, jax.numpy as jnp
        import numpy as np
        HIDDEN = 512
        INTER = 2048
        B, S = (4, 256)

        def _qmatmul(x, w_int8, scale):
            y = jnp.einsum('bsh,ho->bso', x, w_int8.astype(x.dtype))
            return y * scale
        key = jax.random.key(seed)
        ks = jax.random.split(key, 7)
        x = jax.random.normal(ks[0], (B, S, HIDDEN), dtype=jnp.float32)
        w_gate = jax.random.randint(ks[1], (HIDDEN, INTER), -128, 128, dtype=jnp.int32).astype(jnp.int8)
        w_up = jax.random.randint(ks[2], (HIDDEN, INTER), -128, 128, dtype=jnp.int32).astype(jnp.int8)
        w_down = jax.random.randint(ks[3], (INTER, HIDDEN), -128, 128, dtype=jnp.int32).astype(jnp.int8)
        s_gate = jax.random.uniform(ks[4], (INTER,), dtype=jnp.float32) * 0.02 + 0.001
        s_up = jax.random.uniform(ks[5], (INTER,), dtype=jnp.float32) * 0.02 + 0.001
        s_down = jax.random.uniform(ks[6], (HIDDEN,), dtype=jnp.float32) * 0.02 + 0.001
        return {'x': x, 'w_gate': w_gate, 'w_up': w_up, 'w_down': w_down, 's_gate': s_gate, 's_up': s_up, 's_down': s_down}
    _L0_ffn_in = _L0_ffn_setup()
    _d = {'L0_attn_x': _L0_attn_in['x'], 'L0_attn_w_qkv': _L0_attn_in['w_qkv'], 'L0_attn_w_out': _L0_attn_in['w_out'], 'L0_attn_w_c1': _L0_attn_in['w_c1'], 'L0_attn_w_c2': _L0_attn_in['w_c2'], 'L0_ffn_w_gate': _L0_ffn_in['w_gate'], 'L0_ffn_w_up': _L0_ffn_in['w_up'], 'L0_ffn_w_down': _L0_ffn_in['w_down'], 'L0_ffn_s_gate': _L0_ffn_in['s_gate'], 'L0_ffn_s_up': _L0_ffn_in['s_up'], 'L0_ffn_s_down': _L0_ffn_in['s_down']}
    _x0 = _d['L0_attn_x']
    _d['L0_attn_x'] = jax.random.normal(jax.random.fold_in(jax.random.key(seed), 1), (1, 4096, 512), dtype=_x0.dtype)
    del _x0
    return _d

def reference(L0_attn_x, L0_attn_w_qkv, L0_attn_w_out, L0_attn_w_c1, L0_attn_w_c2, L0_ffn_w_gate, L0_ffn_w_up, L0_ffn_w_down, L0_ffn_s_gate, L0_ffn_s_up, L0_ffn_s_down):

    def _L0_attn_ref(x, w_qkv, w_out, w_c1, w_c2):
        import jax, jax.numpy as jnp
        import numpy as np
        EMB = 512
        HEADS = 16
        HEAD_DIM = EMB // HEADS
        MIN_WINDOW = 64
        MAX_WINDOW = 64
        ROPE_BASE = 10000.0

        def _rotate_half(t):
            x1 = t[..., ::2]
            x2 = t[..., 1::2]
            return jnp.stack((-x2, x1), axis=-1).reshape(t.shape)

        def _rope_tables(seq_len, dtype):
            inv_freq = 1.0 / ROPE_BASE ** (jnp.arange(0, HEAD_DIM, 2, dtype=jnp.float32) / HEAD_DIM)
            pos = jnp.arange(seq_len, dtype=jnp.float32)
            freqs = jnp.outer(pos, inv_freq)
            emb = jnp.concatenate([freqs, freqs], axis=-1)
            return (jnp.cos(emb)[None, None].astype(dtype), jnp.sin(emb)[None, None].astype(dtype))

        def _forward(x, w_qkv, w_out, w_c1, w_c2):
            B, S, _ = x.shape
            scale = HEAD_DIM ** (-0.5)
            qkv = x @ w_qkv.T
            qkv = qkv.reshape(B, S, 3, HEADS, HEAD_DIM).transpose(2, 0, 3, 1, 4)
            q, k, v = (qkv[0], qkv[1], qkv[2])
            cos, sin = _rope_tables(S, x.dtype)
            q = q * cos + _rotate_half(q) * sin
            k = k * cos + _rotate_half(k) * sin
            scores = jnp.einsum('bhqd,bhkd->bhqk', q, k) * scale
            var = jnp.var(x.reshape(B, -1), axis=1, ddof=1)
            var_norm = jax.nn.sigmoid(var * 10.0 - 5.0)
            x_mean = x.mean(axis=1)
            hidden = jax.nn.silu(x_mean @ w_c1.T)
            learned = jax.nn.sigmoid(hidden @ w_c2.T)[:, 0]
            complexity = (var_norm + learned) / 2.0
            window_f = MIN_WINDOW + complexity * (MAX_WINDOW - MIN_WINDOW)
            window = window_f.mean().astype(jnp.int32)
            window = jnp.maximum(jnp.minimum(window, S), MIN_WINDOW)
            pos = jnp.arange(S)
            rel = pos[:, None] - pos[None, :]
            keep = (rel >= 0) & (rel < window)
            scores = jnp.where(keep[None, None], scores, -jnp.inf)
            attn = jax.nn.softmax(scores, axis=-1)
            out = jnp.einsum('bhqk,bhkd->bhqd', attn, v)
            out = out.transpose(0, 2, 1, 3).reshape(B, S, EMB)
            return out @ w_out.T
        return _forward(x, w_qkv, w_out, w_c1, w_c2)

    def _L0_ffn_ref(x, w_gate, w_up, w_down, s_gate, s_up, s_down):
        import jax, jax.numpy as jnp
        import numpy as np
        HIDDEN = 512
        INTER = 2048
        B, S = (4, 256)

        def _qmatmul(x, w_int8, scale):
            y = jnp.einsum('bsh,ho->bso', x, w_int8.astype(x.dtype))
            return y * scale
        gate = jax.nn.silu(_qmatmul(x, w_gate, s_gate))
        up = _qmatmul(x, w_up, s_up)
        fuse = gate * up
        return _qmatmul(fuse, w_down, s_down)
    x = L0_attn_x
    x = _layernorm(x + _L0_attn_ref(x, L0_attn_w_qkv, L0_attn_w_out, L0_attn_w_c1, L0_attn_w_c2), axis=-1)
    x = _layernorm(x + _L0_ffn_ref(x, L0_ffn_w_gate, L0_ffn_w_up, L0_ffn_w_down, L0_ffn_s_gate, L0_ffn_s_up, L0_ffn_s_down), axis=-1)
    return x

_drawn_inputs = setup_inputs


def setup_inputs(seed=0):
    import zlib

    import numpy as np

    out = dict(_drawn_inputs(seed))
    spreads = {}
    factors = {}
    for name, (base, spread) in spreads.items():
        noise = np.random.default_rng([zlib.crc32(name.encode()), seed]).standard_normal(out[name].shape)
        drawn = base * np.exp(spread * noise) if base else spread * noise
        out[name] = jnp.asarray(drawn.astype(out[name].dtype))
    for name, factor in factors.items():
        out[name] = (out[name] * factor).astype(out[name].dtype)
    return out
```

```python
from contextlib import ExitStack

import concourse.bass as bass
from concourse import mybir

F32 = mybir.dt.float32
F16 = mybir.dt.float16
BF16 = mybir.dt.bfloat16
I32 = mybir.dt.int32
ALU = mybir.AluOpType
ACT = mybir.ActivationFunctionType
AX = mybir.AxisListType

P = 128
EMB = 512
HEADS = 16
HEAD_DIM = EMB // HEADS
HALF = HEAD_DIM // 2
WINDOW = 64
INTER = 2048
EPS = 1e-5
SCALE = float(HEAD_DIM) ** -0.5

KC = EMB // P
TILE = 512
NB = TILE // P
HG = 4
NG = HEADS // HG
STEPS = NB * NG
X1_SCALE = 2.0 ** 10
MASKED = -(2.0 ** 120)
EXPONENT_BITS = 0x7F800000
assert STEPS == INTER // P and WINDOW * 2 == P


def done(kind, instruction):
    instruction.then_inc(kind[0], 1)


def wait(kind, eng, tile, n):
    sem, per_tile = kind
    value = tile * per_tile + (n + 1)
    if isinstance(value, int) and value <= 0:
        return
    eng.wait_ge(sem, value)


def free_view(ap, dims, offset=0):
    return bass.AP(ap.tensor, ap.offset + offset, [list(ap.ap[0])] + [list(d) for d in dims])


def build(nc, x, xT, w_qkvT, w_outT, w_gate, w_up, w_down, s_gate, s_up, s_down, rope, mask_mid, mask_first,
          eye, out):
    I8 = mybir.dt.int8
    w_gate, w_up, w_down = (w.bitcast(I8) for w in (w_gate, w_up, w_down))
    S = x.shape[0]
    NT = S // TILE
    ctx = ExitStack()
    with ctx:
        def sb(name, shape, dt):
            return ctx.enter_context(nc.sbuf_tensor(name, shape, dt))

        def sem(name):
            return ctx.enter_context(nc.semaphore(name))

        wqkv = sb("wqkv", [P, KC, 3 * EMB], F32)
        wout = sb("wout", [P, KC, EMB], F32)
        wg = sb("wg", [P, KC, INTER], F16)
        wu = sb("wu", [P, KC, INTER], F16)
        wd = sb("wd", [P, STEPS, EMB], F16)
        eye32 = sb("eye32", [P, P], F32)
        eye16 = sb("eye16", [P, P], F16)
        eyeb = sb("eyeb", [P, P], BF16)
        mask_tile = sb("mask_tile", [P, P], BF16)
        mask_start = sb("mask_start", [P, P], BF16)
        sdown = sb("sdown", [P, EMB], F32)
        tanh_scale = sb("tanh_scale", [P, STEPS], F32)
        fuse_scale = sb("fuse_scale", [P, STEPS], F32)
        scales = sb("scales", [P, 16], F32)
        half_power = sb("half_power", [P, 1], F32)

        xT_sb = sb("xT_sb", [P, 2, KC, P], F32)
        tables = sb("tables", [P, NB, 4, HALF], F32)
        qkT = sb("qkT", [P, 2 * NB + 1, HEADS, P], F16)
        v_own = sb("v_own", [P, NB, EMB], F32)
        v_cross = sb("v_cross", [P, NB + 1, EMB], F32)
        probs = sb("probs", [P, HG, P], F32)
        probsT = sb("probsT", [P, HG, P], F32)
        oT = sb("oT", [P, 2, KC, P], F32)
        x1 = sb("x1", [P, NB, EMB], F32)
        x1T = sb("x1T", [P, 2, KC, TILE], F16)
        fuse = sb("fuse", [P, STEPS, 2, TILE], F16)
        ffn_tmp = sb("ffn_tmp", [P, 2, TILE], F32)
        y = sb("y", [P, 2, EMB], F32)
        row_max = sb("row_max", [P, 2, HG], F32)
        neg_max = sb("neg_max", [P, 2, HG], F32)
        row_sum = sb("row_sum", [P, 2, HEADS], F32)
        inv_sum = sb("inv_sum", [P, HEADS], F32)
        stats = sb("stats", [P, 2, 6], F32)
        mean_var = sb("mean_var", [P, 2, 4], F32)
        rstd = sb("rstd", [P, 2], F32)

        x_rows = x1T[:, :, :, :].rearrange("p a k t -> p (a k t)").bitcast(F32).rearrange("p (b n) -> p b n", b=NB)
        fuse32 = fuse[:, :, :, :].rearrange("p s a t -> p (s a t)").bitcast(F32)
        rope_t = [fuse32[:, i * EMB:(i + 1) * EMB] for i in range(4)]
        split_at = 12 * 2 * TILE
        qk_split = fuse[:, :, :, :].rearrange("p s a t -> p (s a t)")[:, split_at:split_at + 2 * HEADS * P]\
            .rearrange("p (z h r d) -> p z h r d", z=2, h=HEADS, r=4)
        x1_split = qkT[:, 2:4, :, :].rearrange("p s h c -> p (s h c)").rearrange("p (b z n) -> p b z n", b=NB, z=2)

        bank = [ctx.enter_context(nc.psum_tensor(f"bank{i}", [P, 512], F32)) for i in range(8)]
        bank32 = [b[:, :] for b in bank]
        bank16 = [b[:, :].bitcast(F16) for b in bank]
        S_BANK, PT_BANK, T_BANK, O_BANK = 4, 5, 6, 7

        def ev(name, per_tile):
            return sem(name), per_tile

        v_done = ev("v_done", NB)
        qk_done = ev("qk_done", NB)
        x1_turned = ev("x1_turned", NB)
        qk_turned = ev("qk_turned", STEPS)
        scores_done = ev("scores_done", STEPS)
        probs_turned = ev("probs_turned", STEPS)
        pv_done = ev("pv_done", STEPS)
        gate_done = ev("gate_done", STEPS)
        up_done = ev("up_done", STEPS)
        o_turned = ev("o_turned", NB)
        down_done = ev("down_done", NB)
        proj_done = ev("proj_done", NB)
        v_kept = ev("v_kept", NB)
        x1T_kept = ev("x1T_kept", NB)
        qk_high = ev("qk_high", NB)
        fuse_high = ev("fuse_high", STEPS)
        exp_done = ev("exp_done", STEPS)
        tanh_done = ev("tanh_done", STEPS)
        probsT_kept = ev("probsT_kept", STEPS)
        oT_kept = ev("oT_kept", NB)
        x1_high = ev("x1_high", NB)
        k_carried = ev("k_carried", 1)
        tables_scaled = ev("tables_scaled", 1)
        rope_read = ev("rope_read", NB)
        rope_done = ev("rope_done", NB)
        qk_low = ev("qk_low", NB)
        qkT_kept = ev("qkT_kept", STEPS)
        max_done = ev("max_done", STEPS)
        bias_done = ev("bias_done", STEPS)
        gated = ev("gated", STEPS)
        fused = ev("fused", STEPS)
        fuse_low = ev("fuse_low", STEPS)
        sum_inverted = ev("sum_inverted", NB)
        o_kept = ev("o_kept", NB)
        down_read = ev("down_read", NB)
        ln2_chain = ev("ln2_chain", 5 * NB)
        y_ready = ev("y_ready", NB)
        proj_read = ev("proj_read", NB)
        ln1_chain = ev("ln1_chain", 4 * NB)
        x1_ready = ev("x1_ready", NB)
        x1_low = ev("x1_low", NB)
        rstd2 = ev("rstd2", NB)
        rstd1 = ev("rstd1", NB)
        xT_in = [sem(f"xT_in{i}") for i in range(2)]
        tables_in = sem("tables_in")
        rows_in = sem("rows_in")
        y_moved = [sem(f"y_moved{i}") for i in range(2)]
        wqkv_in, wout_in, wffn_in, const_in, wd_in = (sem(n) for n in ("wqkv_in", "wout_in", "wffn_in", "const_in", "wd_in"))
        chunk_in = [sem(f"chunk_in{i}") for i in range(4)]
        setup = sem("setup")
        pool_setup = sem("pool_setup")
        consts_ready = sem("consts_ready")

        NCH = 4
        CH = S // P // NCH * EMB
        SLOT = CH
        stage = [fuse32[:, i * SLOT:(i + 1) * SLOT] for i in range(2)]
        raw_const = y[:, :, :].rearrange("p a n -> p (a n)")
        s_raw = ffn_tmp[:, 0, 0:2 * STEPS]
        x_chunks = x.rearrange("(p c r) n -> c p (r n)", p=P, c=NCH)

        def bodies(eng, body):
            body(0, True, False)
            with eng.Fori(1, NT) as t:
                body(t, True, True)
            body(NT, False, True)

        block = ctx.enter_context(nc.Block())

        @block.sync
        def _(sp):
            def load_xT(a, j):
                wait(qk_done, sp, a, j - 2)
                src = xT.rearrange("(k p) s -> p k s", p=P)[:, :, bass.ds(a * TILE + j * P, P)]
                sp.dma_start(xT_sb[:, j % 2, :, :], src).then_inc(xT_in[j % 2], 16)

            sp.dma_start(wqkv[:, :, :], w_qkvT.rearrange("(k p) n -> p k n", p=P)).then_inc(wqkv_in, 16)

            def body(t, attn, ffn):
                if not attn:
                    return
                a = t
                load_xT(a, 0)
                load_xT(a, 1)
                if ffn:
                    wait(rope_read, sp, a - 1, NB - 1)
                src = rope[bass.ds(a * TILE, TILE), :].rearrange("(b p) c -> p b c", p=P)
                sp.dma_start(tables[:, :, :, :].rearrange("p b c i -> p b (c i)"), src).then_inc(tables_in, 16)
                if not ffn:
                    for src, dst in ((s_gate, s_raw[:, 0:STEPS]), (s_up, s_raw[:, STEPS:2 * STEPS]),
                                     (mask_first, raw_const[:, 2 * P:3 * P])):
                        sp.dma_start(dst, src).then_inc(const_in, 16)
                    sp.dma_start(sdown[:, :], s_down.to_broadcast([P, EMB])).then_inc(const_in, 16)
                    for c in range(NCH):
                        if c >= 2:
                            sp.wait_ge(setup, c - 1)
                        sp.dma_start(stage[c % 2], x_chunks[c]).then_inc(chunk_in[c], 16)
                    sp.dma_start(wout[:, :, :], w_outT.rearrange("(k p) n -> p k n", p=P)).then_inc(wout_in, 16)
                load_xT(a, 2)
                load_xT(a, 3)
                if ffn:
                    wait(up_done, sp, t - 1, STEPS - 1)
                src = x[bass.ds(a * TILE, TILE), :].rearrange("(b p) n -> p b n", p=P)
                sp.dma_start(x_rows, src).then_inc(rows_in, 16)

            bodies(sp, body)

        @block.gpsimd
        def _(pool):
            pool.dma_start(raw_const[:, 0:P], eye).then_inc(y_moved[0], 16)
            pool.dma_start(raw_const[:, P:2 * P], mask_mid).then_inc(y_moved[1], 16)
            pool.dma_start(wg[:, :, :], w_gate.rearrange("(k p) n -> p k n", p=P)).then_inc(wffn_in, 16)
            pool.dma_start(wu[:, :, :], w_up.rearrange("(k p) n -> p k n", p=P)).then_inc(wffn_in, 16)
            pool.dma_start(wd[:, :, :], w_down.rearrange("(s p) n -> p s n", p=P)).then_inc(wd_in, 16)
            pool.memset(half_power[:, :], -0.5).then_inc(pool_setup, 1)
            pool.wait_ge(setup, NCH + 3)
            pool.partition_all_reduce(scales[:, 4:7], scales[:, 0:3], P, bass.bass_isa.ReduceOp.absmax)\
                .then_inc(pool_setup, 1)
            pool.wait_ge(pool_setup, 2)

            def body(t, attn, ffn):
                for j in range(NB):
                    if ffn:
                        wait(ln2_chain, pool, t - 1, 5 * j + 4)
                        done(rstd2, pool.tensor_tensor(rstd[:, 1:2], mean_var[:, 1, 1:2], half_power[:, :], ALU.pow))
                    if attn:
                        wait(ln1_chain, pool, t, 4 * j + 3)
                        done(rstd1, pool.tensor_tensor(rstd[:, 0:1], mean_var[:, 0, 1:2], half_power[:, :], ALU.pow))
                    if ffn:
                        wait(y_ready, pool, t - 1, j)
                        dst = out[bass.ds((t - 1) * TILE + j * P, P), :]
                        pool.dma_start(dst, y[:, j % 2, :]).then_inc(y_moved[j % 2], 16)

            bodies(pool, body)
            for i in range(2):
                pool.wait_ge(y_moved[i], 16 * (1 + NT * NB // 2))

        @block.tensor
        def _(pe):
            def product(dst, pairs):
                for i, (lhsT, rhs) in enumerate(pairs):
                    last = pe.matmul(dst, lhsT, rhs, start=(i == 0), stop=(i == len(pairs) - 1))
                return last

            def qkv(j, part, dst):
                cols = slice(part * EMB, (part + 1) * EMB)
                return product(dst, [(xT_sb[:, j % 2, k, :], wqkv[:, k, cols]) for k in range(KC)])

            def turn_qk(a, j, m):
                n = NG * j + m
                last_block = j == NB - 1
                b = T_BANK if last_block else PT_BANK + m % 2
                if m == 0:
                    wait(qk_low, pe, a, j)
                if n < 2:
                    wait(oT_kept, pe, a - 1, NB - 1)
                else:
                    wait(qkT_kept, pe, a, n - 1 if last_block else n - 2)
                for z in range(2):
                    for h in range(HG):
                        src = qk_split[:, z, HG * m + h, :, :].rearrange("p r d -> p (r d)")
                        last = pe.transpose(bank16[b][:, (z * HG + h) * P:(z * HG + h + 1) * P], src, eye16[:, :])
                done(qk_turned, last)

            def scores(t, a, s):
                b, g = s // NG, s % NG
                wait(qkT_kept, pe, a, s)
                if s == 0:
                    wait(k_carried, pe, a, 0)
                    wait(v_kept, pe, a, NB - 1)
                else:
                    wait(exp_done, pe, a, s - 1)
                mask = mask_start if (isinstance(t, int) and t == 0 and b == 0) else mask_tile
                pe.matmul(bank32[S_BANK], eyeb[:, :], free_view(mask[:, :], [[0, HG], [1, P]]), start=True,
                          stop=False, skip_group_check=True)
                for h in range(HG):
                    head = HG * g + h
                    k_block = qkT[:, 2 * NB - 1 - b, head, :]
                    k_first = free_view(k_block, [[HEADS * P + WINDOW, 2], [1, WINDOW]])
                    for half, keys in ((0, k_first), (1, k_block)):
                        rows = slice(half * WINDOW, (half + 1) * WINDOW)
                        last = pe.matmul(bank32[S_BANK][rows, h * P:(h + 1) * P], qkT[:, b, head, rows], keys,
                                         start=False, stop=(h == HG - 1), skip_group_check=True)
                done(scores_done, last)

            def turn_probs(a, s):
                wait(exp_done, pe, a, s)
                if s == 0:
                    wait(qkT_kept, pe, a, NG * (NB - 1) - 2)
                else:
                    wait(probsT_kept, pe, a, s - 1)
                for h in range(HG):
                    last = pe.transpose(bank32[PT_BANK][:, h * P:(h + 1) * P], probs[:, h, :], eye32[:, :])
                done(probs_turned, last)

            def weigh_v(a, s, ffn):
                b, g = s // NG, s % NG
                wait(probsT_kept, pe, a, s)
                if g == 0 and b > 0:
                    wait(o_kept, pe, a, b - 1)
                if s == 0 and ffn:
                    wait(x1T_kept, pe, a - 1, NB - 1)
                for h in range(HG):
                    cols = slice((HG * g + h) * HEAD_DIM, (HG * g + h + 1) * HEAD_DIM)
                    for half, v in ((0, v_cross), (1, v_own)):
                        rows = slice(half * WINDOW, (half + 1) * WINDOW)
                        last = pe.matmul(bank32[O_BANK][rows, cols], probsT[:, h, rows], v[:, b, cols],
                                         start=True, stop=True)
                done(pv_done, last)

            def inner(w, s, dst):
                cols = slice(s * P, (s + 1) * P)
                return product(dst, [(w[:, k, cols], x1T[:, z, k, :]) for k in range(KC) for z in range(2)])

            def body(t, attn, ffn):
                a, f = t, t - 1
                for j in range(NB):
                    if attn:
                        pe.wait_ge(xT_in[j % 2], (a * (NB // 2) + (j // 2 + 1)) * 16)
                        if j == 0:
                            wait(exp_done, pe, a - 1, STEPS - 1)
                        else:
                            wait(v_kept, pe, a, j - 1)
                        done(v_done, qkv(j, 2, bank32[S_BANK]))
                    if ffn:
                        wait(x1_low, pe, f, j)
                        if j == 0:
                            wait(o_kept, pe, f, NB - 1)
                        else:
                            wait(x1T_kept, pe, f, j - 1)
                        for z in range(2):
                            for k in range(KC):
                                c = (z * KC + k) * P
                                last = pe.transpose(bank16[O_BANK][:, c:c + P],
                                                    x1_split[:, j, z, k * P:(k + 1) * P], eye16[:, :])
                        done(x1_turned, last)
                    if attn:
                        if j < 2:
                            wait(proj_read, pe, a - 1, NB - 1)
                        else:
                            wait(rope_read, pe, a, j - 2)
                        qkv(j, 0, bank32[2 * (j % 2)])
                        if j:
                            turn_qk(a, j - 1, 0)
                            turn_qk(a, j - 1, 1)
                        done(qk_done, qkv(j, 1, bank32[2 * (j % 2) + 1]))
                        if j:
                            turn_qk(a, j - 1, 2)
                            turn_qk(a, j - 1, 3)
                for s in range(STEPS):
                    gate_bank, up_bank = bank32[2 * (s % 2)], bank32[2 * (s % 2) + 1]
                    if attn:
                        scores(t, a, s)
                        if s:
                            weigh_v(a, s - 1, ffn)
                    if ffn:
                        if s == 0:
                            wait(x1T_kept, pe, f, NB - 1)
                        if s >= 2:
                            wait(gated, pe, f, s - 2)
                        elif attn:
                            wait(rope_read, pe, a, NB - 2 + s)
                        else:
                            wait(proj_read, pe, a - 1, NB - 1)
                        done(gate_done, inner(wg, s, gate_bank))
                    if attn:
                        turn_probs(a, s)
                    if ffn:
                        if s >= 2:
                            wait(fused, pe, f, s - 2)
                        done(up_done, inner(wu, s, up_bank))
                    if attn and 2 <= s < 2 + NG:
                        turn_qk(a, NB - 1, s - 2)
                if attn:
                    weigh_v(a, STEPS - 1, ffn)
                for j in range(NB):
                    if attn:
                        wait(o_kept, pe, a, j)
                        if j == 0:
                            wait(probsT_kept, pe, a, STEPS - 1)
                        elif j == 1:
                            wait(qkT_kept, pe, a, STEPS - 1)
                        else:
                            wait(oT_kept, pe, a, j - 2)
                        for k in range(KC):
                            last = pe.transpose(bank32[PT_BANK + j % 2][:, k * P:(k + 1) * P],
                                                v_own[:, j, k * P:(k + 1) * P], eye32[:, :])
                        done(o_turned, last)
                    if ffn:
                        if j < 2:
                            wait(fuse_low, pe, f, STEPS - 2)
                        else:
                            wait(down_read, pe, f, j - 2)
                        rows = slice(j * P, (j + 1) * P)
                        for s in range(STEPS):
                            if j == 0 and s == STEPS - 1:
                                wait(fuse_low, pe, f, STEPS - 1)
                            for z in range(2):
                                last = pe.matmul(bank32[j % 2], fuse[:, s, z, rows], wd[:, s, :],
                                                 start=(s == 0 and z == 0), stop=(s == STEPS - 1 and z == 1))
                        done(down_done, last)
                    if attn:
                        wait(oT_kept, pe, a, j)
                        if j < 2:
                            if ffn:
                                wait(fused, pe, f, STEPS - 1)
                            else:
                                wait(rope_read, pe, a, NB - 1)
                        else:
                            wait(proj_read, pe, a, j - 2)
                        done(proj_done, product(bank32[2 + j % 2],
                                                 [(oT[:, j % 2, k, :], wout[:, k, :]) for k in range(KC)]))

            pe.wait_ge(wqkv_in, 16)
            pe.wait_ge(consts_ready, 1)
            body(0, True, False)
            pe.wait_ge(wffn_in, 32)
            pe.wait_ge(wd_in, 16)
            with pe.Fori(1, NT) as t:
                body(t, True, True)
            body(NT, False, True)

        @block.scalar
        def _(act):
            def copy(dst, src, scale=1.0):
                return act.activation(dst, src, ACT.Copy, scale=scale)

            def keep_fuse_high(f, s):
                wait(fused, act, f, s)
                done(fuse_high, copy(fuse[:, s, 0, :], ffn_tmp[:, s % 2, :]))

            def body(t, attn, ffn):
                a, f = t, t - 1
                for j in range(NB):
                    if attn:
                        if ffn:
                            wait(o_turned, act, a - 1, j)
                        if j == 0 and ffn:
                            wait(v_kept, act, a - 1, NB - 1)
                            copy(v_cross[WINDOW:P, 0, :], v_cross[WINDOW:P, NB, :])
                        wait(v_done, act, a, j)
                        copy(v_own[:, j, :], bank32[S_BANK])
                        copy(v_cross[0:WINDOW, j, :], bank32[S_BANK][0:WINDOW, :])
                        done(v_kept, copy(v_cross[WINDOW:P, j + 1, :], bank32[S_BANK][WINDOW:P, :]))
                    if ffn:
                        wait(x1_turned, act, f, j)
                        if j == 0:
                            wait(proj_read, act, f, NB - 1)
                        done(x1T_kept, copy(x1T[:, :, :, j * P:(j + 1) * P],
                                             bank16[O_BANK].rearrange("p (z k c) -> p z k c", z=2, k=KC)))
                    if attn:
                        wait(rope_done, act, a, j)
                        wait(qk_turned, act, a, NG * j - 1)
                        for z in range(2):
                            for odd in range(2):
                                src = free_view(rope_t[2 * odd], [[HALF, HEADS], [0, 2], [1, HALF]], z * EMB // 2)
                                twice = slice(0, 2) if z == 0 else slice(0, 4, 2)
                                last = copy(qk_split[:, z, :, twice, odd * HALF:(odd + 1) * HALF], src)
                        done(qk_high, last)
                for s in range(STEPS):
                    b, g = s // NG, s % NG
                    if ffn and s:
                        keep_fuse_high(f, s - 1)
                    if attn:
                        wait(bias_done, act, a, s)
                        wait(probs_turned, act, a, s - 1)
                        if g == 0:
                            wait(o_kept, act, a, b - 2)
                        for h in range(HG):
                            last = act.activation(probs[:, h, :], bank32[S_BANK][:, h * P:(h + 1) * P], ACT.Exp,
                                                  bias=neg_max[:, s % 2, h:h + 1], scale=scales[:, 10:11],
                                                  accum_out=row_sum[:, b % 2, HG * g + h:HG * g + h + 1])
                        done(exp_done, last)
                    if ffn:
                        wait(gate_done, act, f, s)
                        if s >= 2:
                            wait(fuse_low, act, f, s - 2)
                        done(tanh_done, act.activation(ffn_tmp[:, s % 2, :], bank32[2 * (s % 2)], ACT.Tanh,
                                                        scale=tanh_scale[:, s:s + 1]))
                    if attn:
                        wait(probs_turned, act, a, s)
                        wait(pv_done, act, a, s - 1)
                        done(probsT_kept, copy(probsT[:, :, :].rearrange("p h c -> p (h c)"), bank32[PT_BANK]))
                if ffn:
                    keep_fuse_high(f, STEPS - 1)
                if attn:
                    for j in range(NB):
                        wait(o_turned, act, a, j)
                        wait(proj_done, act, a, j - 2)
                        done(oT_kept, copy(oT[:, j % 2, :, :].rearrange("p k c -> p (k c)"),
                                            bank32[PT_BANK + j % 2]))
                        wait(x1_ready, act, a, j)
                        done(x1_high, copy(x1_split[:, j, 0, :], x1[:, j, :], X1_SCALE))

            act.wait_ge(consts_ready, 1)
            bodies(act, body)

        @block.vector
        def _(dve):
            def keep_qkT(a, j, m):
                n = NG * j + m
                wait(qk_turned, dve, a, n)
                b = T_BANK if j == NB - 1 else PT_BANK + m % 2
                k_slot = 2 * NB - 1 - j
                dst = free_view(qkT[:, j, HG * m, :], [[(k_slot - j) * HEADS * P, 2], [1, HG * P]])
                done(qkT_kept, dve.tensor_copy(dst, bank16[b].rearrange("p (z c) -> p z c", z=2)))

            def rope_block(a, j):
                even, odd = bank32[2 * (j % 2)], bank32[2 * (j % 2) + 1]
                heads = [[HALF, 2 * HEADS], [1, HALF]]

                def table(i):
                    return free_view(tables[:, j, i, :], [[0, 2 * HEADS], [1, HALF]])

                wait(qk_done, dve, a, j)
                wait(qk_high, dve, a, j - 1)
                for i, src in enumerate((even, odd, odd, even)):
                    last = dve.tensor_tensor(free_view(rope_t[i], heads), free_view(src, heads), table(i), ALU.mult)
                done(rope_read, last)
                wait(rope_read, dve, a, j)
                dve.tensor_tensor(rope_t[0], rope_t[0], rope_t[1], ALU.subtract)
                done(rope_done, dve.tensor_tensor(rope_t[2], rope_t[2], rope_t[3], ALU.add))

            def split_low(a, j):
                wait(qk_high, dve, a, j)
                for z in range(2):
                    for odd in range(2):
                        part = slice(odd * HALF, (odd + 1) * HALF)
                        src = free_view(rope_t[2 * odd], [[HALF, HEADS], [0, 2], [1, HALF]], z * EMB // 2)
                        high = free_view(qk_split[:, z, 0, 0, part], [[P, HEADS], [0, 2], [1, HALF]])
                        twice = slice(2, 4) if z == 0 else slice(1, 4, 2)
                        last = dve.tensor_tensor(qk_split[:, z, :, twice, part], src, high, ALU.subtract)
                done(qk_low, last)

            def normalise_o(a, b):
                wait(pv_done, dve, a, NG * (b + 1) - 1)
                done(sum_inverted, dve.reciprocal(inv_sum[:, :], row_sum[:, b % 2, :]))
                wait(sum_inverted, dve, a, b)
                view = [[HEAD_DIM, HEADS], [1, HEAD_DIM]]
                done(o_kept, dve.tensor_tensor(free_view(v_own[:, b, :], view), free_view(bank32[O_BANK], view),
                                                free_view(inv_sum[:, :], [[1, HEADS], [0, HEAD_DIM]]), ALU.mult))

            def keep_fuse_low(f, s):
                wait(fuse_high, dve, f, s)
                done(fuse_low, dve.tensor_tensor(fuse[:, s, 1, :], ffn_tmp[:, s % 2, :], fuse[:, s, 0, :],
                                                  ALU.subtract))

            def moments(chain, tile, first, rows, z):
                st, mv = stats[:, z, :], mean_var[:, z, :]
                done(chain, dve.bn_stats(st, rows))
                wait(chain, dve, tile, first)
                dve.tensor_tensor(mv[:, 0:2], st[:, 1:3], st[:, 4:6], ALU.add)
                done(chain, dve.tensor_tensor(mv[:, 2:3], st[:, 1:2], st[:, 4:5], ALU.subtract))
                wait(chain, dve, tile, first + 1)
                dve.tensor_scalar(mv[:, 0:1], mv[:, 0:1], 0.5, None, ALU.mult)
                dve.scalar_tensor_tensor(out=mv[:, 3:4], in0=mv[:, 2:3], scalar=0.25, in1=mv[:, 2:3],
                                         op0=ALU.mult, op1=ALU.mult)
                done(chain, dve.tensor_scalar(mv[:, 1:2], mv[:, 1:2], 1.0 / EMB, EPS, ALU.mult, ALU.add))
                wait(chain, dve, tile, first + 2)
                done(chain, dve.tensor_tensor(mv[:, 1:2], mv[:, 1:2], mv[:, 3:4], ALU.add))

            def body(t, attn, ffn):
                a, f = t, t - 1
                if attn:
                    before = qkT[:, 2 * NB, :, WINDOW:P]
                    if ffn:
                        wait(qkT_kept, dve, a - 1, STEPS - 1)
                        done(k_carried, dve.tensor_copy(before, qkT[:, NB, :, WINDOW:P]))
                    else:
                        done(k_carried, dve.memset(before, 0.0))
                    dve.wait_ge(tables_in, (a + 1) * 16)
                    flat = tables[:, :, :, :].rearrange("p b c i -> p (b c i)")
                    done(tables_scaled, dve.tensor_scalar(flat, flat, scales[:, 9:10], None, ALU.mult))
                    wait(tables_scaled, dve, a, 0)
                    for j in range(NB):
                        if j:
                            for m in range(NG):
                                keep_qkT(a, j - 1, m)
                        rope_block(a, j)
                        split_low(a, j)
                for s in range(STEPS):
                    if attn:
                        wait(scores_done, dve, a, s)
                        done(max_done, dve.tensor_reduce(row_max[:, s % 2, :],
                                                          bank32[S_BANK].rearrange("p (h c) -> p h c", h=HG),
                                                          AX.X, ALU.max))
                        wait(max_done, dve, a, s)
                        done(bias_done, dve.tensor_scalar(neg_max[:, s % 2, :], row_max[:, s % 2, :],
                                                           scales[:, 11:12], None, ALU.mult))
                    if ffn and s:
                        keep_fuse_low(f, s - 1)
                    if attn and s and s % NG == 0:
                        normalise_o(a, s // NG - 1)
                    if ffn:
                        tmp = ffn_tmp[:, s % 2, :]
                        wait(tanh_done, dve, f, s)
                        done(gated, dve.scalar_tensor_tensor(out=tmp, in0=tmp, scalar=1.0, in1=bank32[2 * (s % 2)],
                                                              op0=ALU.add, op1=ALU.mult))
                        wait(up_done, dve, f, s)
                        wait(gated, dve, f, s)
                        done(fused, dve.scalar_tensor_tensor(out=tmp, in0=bank32[2 * (s % 2) + 1],
                                                              scalar=fuse_scale[:, s:s + 1], in1=tmp,
                                                              op0=ALU.mult, op1=ALU.mult))
                    if attn and 2 <= s < 2 + NG:
                        keep_qkT(a, NB - 1, s - 2)
                if attn:
                    normalise_o(a, NB - 1)
                if ffn:
                    keep_fuse_low(f, STEPS - 1)
                for j in range(NB):
                    rows_y, rows_x1 = y[:, j % 2, :], x1[:, j, :]
                    if ffn:
                        wait(down_done, dve, f, j)
                        dve.wait_ge(y_moved[j % 2], (f * (NB // 2) + (j // 2 + 1)) * 16)
                        done(down_read, dve.tensor_tensor(rows_y, bank32[j % 2], sdown[:, :], ALU.mult))
                        wait(down_read, dve, f, j)
                        done(ln2_chain, dve.tensor_tensor(rows_y, rows_y, rows_x1, ALU.add))
                        wait(ln2_chain, dve, f, 5 * j)
                        moments(ln2_chain, f, 5 * j + 1, rows_y, 1)
                    if attn:
                        if j == 0:
                            dve.wait_ge(rows_in, (a + 1) * 16)
                        wait(proj_done, dve, a, j)
                        done(proj_read, dve.tensor_tensor(rows_x1, bank32[2 + j % 2], x_rows[:, j, :], ALU.add))
                        wait(proj_read, dve, a, j)
                        moments(ln1_chain, a, 4 * j, rows_x1, 0)
                    if ffn:
                        wait(rstd2, dve, f, j)
                        done(y_ready, dve.tensor_scalar(rows_y, rows_y, mean_var[:, 1, 0:1], rstd[:, 1:2],
                                                         ALU.subtract, ALU.mult))
                    if attn:
                        wait(rstd1, dve, a, j)
                        done(x1_ready, dve.tensor_scalar(rows_x1, rows_x1, mean_var[:, 0, 0:1], rstd[:, 0:1],
                                                          ALU.subtract, ALU.mult))
                        wait(x1_high, dve, a, j)
                        done(x1_low, dve.scalar_tensor_tensor(out=x1_split[:, j, 1, :], in0=rows_x1, scalar=X1_SCALE,
                                                               in1=x1_split[:, j, 0, :], op0=ALU.mult,
                                                               op1=ALU.subtract))

            dve.memset(v_cross[WINDOW:P, 0, :], 0.0)
            dve.wait_ge(const_in, 4 * 16)
            for i in range(2):
                dve.wait_ge(y_moved[i], 16)
            dve.tensor_copy(eye32[:, :], raw_const[:, 0:P])
            dve.tensor_copy(eye16[:, :], raw_const[:, 0:P])
            dve.tensor_copy(eyeb[:, :], raw_const[:, 0:P])
            dve.tensor_copy(mask_tile[:, :], raw_const[:, P:2 * P])
            dve.tensor_copy(mask_start[:, :], raw_const[:, 2 * P:3 * P])
            dve.tensor_scalar(tanh_scale[:, :], s_raw[:, 0:STEPS], 0.5 / X1_SCALE, None, ALU.mult)
            dve.tensor_tensor(fuse_scale[:, :], s_raw[:, 0:STEPS], s_raw[:, STEPS:2 * STEPS], ALU.mult)\
                .then_inc(consts_ready, 1)
            for c in range(NCH):
                dve.wait_ge(chunk_in[c], 16)
                dve.tensor_reduce(scales[:, 12 + c:13 + c], stage[c % 2], AX.X, ALU.max,
                                  apply_absolute_value=True).then_inc(setup, 1)
            dve.wait_ge(wqkv_in, 16)
            dve.tensor_reduce(scales[:, 1:2], wqkv[:, :, :].rearrange("p k n -> p (k n)"), AX.X, ALU.max,
                              apply_absolute_value=True).then_inc(setup, 1)
            dve.wait_ge(consts_ready, 1)
            dve.tensor_reduce(scales[:, 2:3], fuse_scale[:, :], AX.X, ALU.max,
                              apply_absolute_value=True).then_inc(setup, 1)
            dve.wait_ge(setup, NCH)
            dve.tensor_reduce(scales[:, 0:1], scales[:, 12:12 + NCH], AX.X, ALU.max).then_inc(setup, 1)
            dve.wait_ge(pool_setup, 2)
            count = [NCH + 3]

            def chained(instruction):
                count[0] += 1
                instruction.then_inc(setup, 1)
                dve.wait_ge(setup, count[0])

            big = scales[:, 4:7]
            chained(dve.tensor_scalar(big, big, 1e-12, None, ALU.max))
            chained(dve.tensor_scalar(big.bitcast(I32), big.bitcast(I32), EXPONENT_BITS, None, ALU.bitwise_and))
            chained(dve.tensor_tensor(scales[:, 7:8], scales[:, 4:5], scales[:, 5:6], ALU.mult))
            chained(dve.tensor_scalar(scales[:, 7:8], scales[:, 7:8], 0.125, None, ALU.mult))
            chained(dve.reciprocal(scales[:, 9:10], scales[:, 7:8]))
            chained(dve.tensor_scalar(scales[:, 10:11], scales[:, 7:8], scales[:, 7:8], SCALE, ALU.mult, ALU.mult))
            chained(dve.tensor_scalar(scales[:, 11:12], scales[:, 10:11], -1.0, None, ALU.mult))
            chained(dve.reciprocal(scales[:, 8:9], scales[:, 6:7]))
            chained(dve.tensor_scalar(fuse_scale[:, :], fuse_scale[:, :], scales[:, 8:9],
                                      0.5 * 2.0 ** -18 / X1_SCALE ** 2, ALU.mult, ALU.mult))
            chained(dve.tensor_scalar(sdown[:, :], sdown[:, :], scales[:, 6:7], 2.0 ** 18, ALU.mult, ALU.mult))
            bodies(dve, body)


_OUT = (1, 4096, 512)


def kernel(L0_attn_x, L0_attn_w_qkv, L0_attn_w_out, L0_attn_w_c1, L0_attn_w_c2, L0_ffn_w_gate, L0_ffn_w_up,
           L0_ffn_w_down, L0_ffn_s_gate, L0_ffn_s_up, L0_ffn_s_down):
    import numpy as np
    import concourse.bacc as bacc
    from concourse.bass_utils import run_bass_kernel_spmd

    x = np.asarray(L0_attn_x)[0]
    n_rows = x.shape[0]
    w = np.asarray(L0_attn_w_qkv)
    q, k, v = w[0:EMB], w[EMB:2 * EMB], w[2 * EMB:3 * EMB]
    w_qkvT = np.ascontiguousarray(np.concatenate([q[0::2], k[0::2], q[1::2], k[1::2], v], axis=0).T)

    inv_freq = np.float32(1.0) / np.power(np.float32(10000.0),
                                          np.arange(0, HEAD_DIM, 2, dtype=np.float32) / np.float32(HEAD_DIM))
    freqs = np.outer(np.arange(n_rows, dtype=np.float32), inv_freq.astype(np.float32))
    cos, sin = np.cos(freqs), np.sin(freqs)
    even = np.arange(0, HEAD_DIM, 2) % HALF
    odd = np.arange(1, HEAD_DIM, 2) % HALF
    rope = np.concatenate([cos[:, even], sin[:, even], cos[:, odd], sin[:, odd]], axis=1).astype(np.float32)

    row, key = np.arange(WINDOW)[:, None], np.arange(WINDOW)[None, :]
    own = np.where(key <= row, 0.0, MASKED)
    earlier = np.where(key > row, 0.0, MASKED)
    nothing = np.full((WINDOW, WINDOW), MASKED)
    mask_mid = np.block([[own, earlier], [earlier, own]]).astype(np.float32)
    mask_first = np.block([[own, nothing], [earlier, own]]).astype(np.float32)

    arrays = {
        "x": x,
        "xT": np.ascontiguousarray(x.T),
        "w_qkvT": w_qkvT,
        "w_outT": np.ascontiguousarray(np.asarray(L0_attn_w_out).T),
        "w_gate": np.ascontiguousarray(L0_ffn_w_gate).view(np.int32),
        "w_up": np.ascontiguousarray(L0_ffn_w_up).view(np.int32),
        "w_down": np.ascontiguousarray(L0_ffn_w_down).view(np.int32),
        "s_gate": np.ascontiguousarray(np.asarray(L0_ffn_s_gate).reshape(STEPS, P).T),
        "s_up": np.ascontiguousarray(np.asarray(L0_ffn_s_up).reshape(STEPS, P).T),
        "s_down": np.ascontiguousarray(np.asarray(L0_ffn_s_down).reshape(1, EMB)),
        "rope": rope,
        "mask_mid": mask_mid,
        "mask_first": mask_first,
        "eye": np.eye(P, dtype=np.float32),
    }
    nc = bacc.Bacc("TRN2", target_bir_lowering=False, num_devices=1)
    args = [nc.dram_tensor(n, a.shape, mybir.dt.from_np(a.dtype), kind="ExternalInput").ap()
            for n, a in arrays.items()]
    out = nc.dram_tensor("out", (n_rows, EMB), F32, kind="ExternalOutput").ap()
    build(nc, *args, out)
    result = run_bass_kernel_spmd(nc, [arrays], core_ids=[0])
    return result.results[0]["out"].reshape(_OUT)
```

```python
from contextlib import ExitStack

import concourse.bass as bass
from concourse import mybir

F32 = mybir.dt.float32
F16 = mybir.dt.float16
BF16 = mybir.dt.bfloat16
I32 = mybir.dt.int32
ALU = mybir.AluOpType
ACT = mybir.ActivationFunctionType
AX = mybir.AxisListType

P = 128
EMB = 512
HEADS = 16
HEAD_DIM = EMB // HEADS
HALF = HEAD_DIM // 2
WINDOW = 64
INTER = 2048
EPS = 1e-5
SCALE = float(HEAD_DIM) ** -0.5

KC = EMB // P
TILE = 512
NB = TILE // P
HG = 4
NG = HEADS // HG
STEPS = NB * NG
X1_SCALE = 2.0 ** 10
MASKED = -(2.0 ** 120)
EXPONENT_BITS = 0x7F800000
SPLIT_FROM = 2
TURN_AT = 6
assert STEPS == INTER // P and WINDOW * 2 == P


def done(kind, instruction):
    instruction.then_inc(kind[0], 1)


def wait(kind, eng, tile, n):
    sem, per_tile = kind
    value = tile * per_tile + (n + 1)
    if isinstance(value, int) and value <= 0:
        return
    eng.wait_ge(sem, value)


def free_view(ap, dims, offset=0):
    return bass.AP(ap.tensor, ap.offset + offset, [list(ap.ap[0])] + [list(d) for d in dims])


def build(nc, x, xT, w_qkvT, w_outT, w_gate, w_up, w_down, s_gate, s_up, s_down, rope, mask_mid, mask_first,
          eye, out):
    I8 = mybir.dt.int8
    w_gate, w_up, w_down = (w.bitcast(I8) for w in (w_gate, w_up, w_down))
    S = x.shape[0]
    NT = S // TILE
    ctx = ExitStack()
    with ctx:
        def sb(name, shape, dt):
            return ctx.enter_context(nc.sbuf_tensor(name, shape, dt))

        def sem(name):
            return ctx.enter_context(nc.semaphore(name))

        wqkv = sb("wqkv", [P, KC, 3 * EMB], F32)
        wout = sb("wout", [P, KC, EMB], F32)
        wg = sb("wg", [P, KC, INTER], F16)
        wu = sb("wu", [P, KC, INTER], F16)
        wd = sb("wd", [P, STEPS, EMB], F16)
        eye32 = sb("eye32", [P, P], F32)
        eye16 = sb("eye16", [P, P], F16)
        mask_tile = sb("mask_tile", [P, P], BF16)
        mask_start = sb("mask_start", [P, P], BF16)
        sdown = sb("sdown", [P, EMB], F32)
        tanh_scale = sb("tanh_scale", [P, STEPS], F32)
        fuse_scale = sb("fuse_scale", [P, STEPS], F32)
        scales = sb("scales", [P, 12], F32)
        chunk_max = sb("chunk_max", [P, 8], F32)
        half_power = sb("half_power", [P, 1], F32)

        xT_sb = sb("xT_sb", [P, 2, KC, P], F32)
        tables = sb("tables", [P, NB, 4, HALF], F32)
        qkT = sb("qkT", [P, 2 * NB + 1, HEADS, P], F16)
        v_own = sb("v_own", [P, NB, EMB], F32)
        v_cross = sb("v_cross", [P, NB + 1, EMB], F32)
        probs = sb("probs", [P, HG, P], F32)
        probsT = sb("probsT", [P, HG, P], F32)
        oT = sb("oT", [P, 2, KC, P], F32)
        x1 = sb("x1", [P, NB, EMB], F32)
        x1T = sb("x1T", [P, 2, KC, TILE], F16)
        fuse = sb("fuse", [P, STEPS, 2, TILE], F16)
        ffn_tmp = sb("ffn_tmp", [P, 2, TILE], F32)
        y = sb("y", [P, 2, EMB], F32)
        row_max = sb("row_max", [P, 2, HG], F32)
        neg_max = sb("neg_max", [P, 2, HG], F32)
        row_sum = sb("row_sum", [P, 2, HEADS], F32)
        inv_sum = sb("inv_sum", [P, HEADS], F32)
        stats = sb("stats", [P, 2, 6], F32)
        mean_var = sb("mean_var", [P, 2, 4], F32)
        rstd = sb("rstd", [P, 2], F32)

        x_rows = x1T[:, :, :, :].rearrange("p a k t -> p (a k t)").bitcast(F32).rearrange("p (b n) -> p b n", b=NB)
        fuse32 = fuse[:, :, :, :].rearrange("p s a t -> p (s a t)").bitcast(F32)
        ROPE_AT, SPLIT_AT = 8, 12
        rope_t = [fuse32[:, (ROPE_AT + i) * EMB:(ROPE_AT + i + 1) * EMB] for i in range(4)]
        split_at = SPLIT_AT * 2 * TILE
        qk_split = fuse[:, :, :, :].rearrange("p s a t -> p (s a t)")[:, split_at:split_at + 2 * HEADS * P]\
            .rearrange("p (z h r d) -> p z h r d", z=2, h=HEADS, r=4)
        x1_split = qkT[:, 2:4, :, :].rearrange("p s h c -> p (s h c)").rearrange("p (b z n) -> p b z n", b=NB, z=2)

        bank = [ctx.enter_context(nc.psum_tensor(f"bank{i}", [P, 512], F32)) for i in range(8)]
        bank32 = [b[:, :] for b in bank]
        bank16 = [b[:, :].bitcast(F16) for b in bank]
        S_BANK, PT_BANK, T_BANK, O_BANK = 4, 5, 6, 7
        TURN_BANKS = (PT_BANK, T_BANK, O_BANK, PT_BANK)

        def ev(name, per_tile):
            return sem(name), per_tile

        v_done = ev("v_done", NB)
        qk_done = ev("qk_done", NB)
        x1_turned = ev("x1_turned", NB)
        qk_turned = ev("qk_turned", STEPS)
        scores_done = ev("scores_done", STEPS)
        probs_turned = ev("probs_turned", STEPS)
        pv_done = ev("pv_done", STEPS)
        gate_done = ev("gate_done", STEPS)
        up_done = ev("up_done", STEPS)
        o_turned = ev("o_turned", NB)
        down_done = ev("down_done", NB)
        proj_done = ev("proj_done", NB)
        v_kept = ev("v_kept", NB)
        x1T_kept = ev("x1T_kept", NB)
        qk_high = ev("qk_high", 4 * NB)
        fuse_high = ev("fuse_high", STEPS)
        qkT_kept_s = ev("qkT_kept_s", 2 * (NB - 1))
        exp_done = ev("exp_done", 2 * STEPS)
        tanh_done = ev("tanh_done", STEPS)
        probsT_kept = ev("probsT_kept", STEPS)
        oT_kept = ev("oT_kept", NB)
        x1_high = ev("x1_high", NB)
        k_carried = ev("k_carried", 1)
        tables_scaled = ev("tables_scaled", 1)
        rope_read = ev("rope_read", NB)
        rope_done = ev("rope_done", NB)
        qk_low = ev("qk_low", NB)
        qkT_kept_v = ev("qkT_kept_v", 2 * (NB - 1) + NG)
        max_done = ev("max_done", STEPS)
        bias_done = ev("bias_done", STEPS)
        gated = ev("gated", STEPS)
        fused = ev("fused", STEPS)
        fuse_low = ev("fuse_low", STEPS)
        sum_inverted = ev("sum_inverted", NB)
        o_kept = ev("o_kept", NB)
        down_read = ev("down_read", NB)
        ln2_chain = ev("ln2_chain", 5 * NB)
        y_ready = ev("y_ready", NB)
        proj_read = ev("proj_read", NB)
        ln1_chain = ev("ln1_chain", 4 * NB)
        x1_ready = ev("x1_ready", NB)
        x1_low = ev("x1_low", NB)
        rstd2 = ev("rstd2", NB)
        rstd1 = ev("rstd1", NB)
        xT_in = [sem(f"xT_in{i}") for i in range(2)]
        tables_in = sem("tables_in")
        rows_in = sem("rows_in")
        y_moved = [sem(f"y_moved{i}") for i in range(2)]
        wout_in, wffn_in, const_in, sdown_in = sem("wout_in"), sem("wffn_in"), sem("const_in"), sem("sdown_in")
        wqkv_in = [sem(f"wqkv_in{i}") for i in range(3)]
        setup = sem("setup")
        pool_setup = sem("pool_setup")
        consts_ready = sem("consts_ready")

        NCH = 8
        CH = S // P // NCH * EMB
        chunk_in = [sem(f"chunk_in{i}") for i in range(NCH)]
        qkT32 = qkT[:, 0:2 * NB, :, :].rearrange("p s h c -> p (s h c)").bitcast(F32)
        stage = [place[:, i * CH:(i + 1) * CH] for place in (fuse32, qkT32) for i in range(NCH // 2)]
        raw_const = y[:, :, :].rearrange("p a n -> p (a n)")
        s_raw = ffn_tmp[:, 0, 0:2 * STEPS]
        x_chunks = x.rearrange("(p c r) n -> c p (r n)", p=P, c=NCH)

        def wait_qkT(eng, a, j, m):
            if j == NB - 1:
                wait(qkT_kept_v, eng, a, 2 * j + m)
            else:
                wait(qkT_kept_s if m % 2 else qkT_kept_v, eng, a, 2 * j + m // 2)

        def turned_qk(j, m):
            b = T_BANK if j == NB - 1 else TURN_BANKS[m]
            q_slot, k_slot = j, 2 * NB - 1 - j
            dst = free_view(qkT[:, q_slot, HG * m, :], [[(k_slot - q_slot) * HEADS * P, 2], [1, HG * P]])
            return dst, bank16[b].rearrange("p (z c) -> p z c", z=2)

        def probs_place(s, ffn):
            return probs[:, :, :] if ffn or s % 2 == 0 else ffn_tmp[:, 1, :].rearrange("p (h c) -> p h c", h=HG)

        def x1_bank(j, attn):
            return O_BANK if attn or j % 2 == 0 else T_BANK

        def score_bank(s, ffn):
            return S_BANK if ffn or s % 2 == 0 else 0

        def bodies(eng, body):
            body(0, True, False)
            with eng.Fori(1, NT) as t:
                body(t, True, True)
            body(NT, False, True)

        block = ctx.enter_context(nc.Block())

        @block.sync
        def _(sp):
            def load_xT(a, j):
                wait(qk_done, sp, a, j - 2)
                src = xT.rearrange("(k p) s -> p k s", p=P)[:, :, bass.ds(a * TILE + j * P, P)]
                sp.dma_start(xT_sb[:, j % 2, :, :], src).then_inc(xT_in[j % 2], 16)

            def load_wqkv(part):
                cols = slice(part * EMB, (part + 1) * EMB)
                sp.dma_start(wqkv[:, :, cols], w_qkvT.rearrange("(k p) n -> p k n", p=P)[:, :, cols])\
                    .then_inc(wqkv_in[part], 16)

            load_wqkv(2)

            def body(t, attn, ffn):
                if not attn:
                    return
                a = t
                load_xT(a, 0)
                if not ffn:
                    for src, dst in ((s_gate, s_raw[:, 0:STEPS]), (s_up, s_raw[:, STEPS:2 * STEPS]),
                                     (mask_first, raw_const[:, 2 * P:3 * P])):
                        sp.dma_start(dst, src).then_inc(const_in, 16)
                    load_wqkv(0)
                    load_wqkv(1)
                load_xT(a, 1)
                if not ffn:
                    for c in range(NCH):
                        sp.dma_start(stage[c], x_chunks[c]).then_inc(chunk_in[c], 16)
                else:
                    wait(rope_read, sp, a - 1, NB - 1)
                src = rope[bass.ds(a * TILE, TILE), :].rearrange("(b p) c -> p b c", p=P)
                sp.dma_start(tables[:, :, :, :].rearrange("p b c i -> p b (c i)"), src).then_inc(tables_in, 16)
                if not ffn:
                    sp.dma_start(sdown[:, :], s_down.to_broadcast([P, EMB])).then_inc(sdown_in, 16)
                load_xT(a, 2)
                load_xT(a, 3)
                if ffn:
                    wait(up_done, sp, t - 1, STEPS - 1)
                src = x[bass.ds(a * TILE, TILE), :].rearrange("(b p) n -> p b n", p=P)
                sp.dma_start(x_rows, src).then_inc(rows_in, 16)
                if not ffn:
                    sp.dma_start(wout[:, :, :], w_outT.rearrange("(k p) n -> p k n", p=P)).then_inc(wout_in, 16)

            bodies(sp, body)

        @block.gpsimd
        def _(pool):
            pool.dma_start(raw_const[:, 0:P], eye).then_inc(y_moved[0], 16)
            pool.dma_start(raw_const[:, P:2 * P], mask_mid).then_inc(y_moved[1], 16)
            pool.memset(half_power[:, :], -0.5).then_inc(pool_setup, 1)
            pool.wait_ge(setup, NCH + 4)
            pool.partition_all_reduce(scales[:, 4:7], scales[:, 0:3], P, bass.bass_isa.ReduceOp.absmax)\
                .then_inc(pool_setup, 1)
            pool.wait_ge(pool_setup, 2)
            pool.dma_start(wg[:, :, :], w_gate.rearrange("(k p) n -> p k n", p=P)).then_inc(wffn_in, 16)
            pool.dma_start(wu[:, :, :], w_up.rearrange("(k p) n -> p k n", p=P)).then_inc(wffn_in, 16)
            pool.dma_start(wd[:, :, :], w_down.rearrange("(s p) n -> p s n", p=P)).then_inc(wffn_in, 16)

            def body(t, attn, ffn):
                for j in range(NB):
                    if ffn:
                        wait(ln2_chain, pool, t - 1, 5 * j + 4)
                        done(rstd2, pool.tensor_tensor(rstd[:, 1:2], mean_var[:, 1, 1:2], half_power[:, :], ALU.pow))
                    if attn:
                        wait(ln1_chain, pool, t, 4 * j + 3)
                        done(rstd1, pool.tensor_tensor(rstd[:, 0:1], mean_var[:, 0, 1:2], half_power[:, :], ALU.pow))
                    if ffn:
                        wait(y_ready, pool, t - 1, j)
                        dst = out[bass.ds((t - 1) * TILE + j * P, P), :]
                        pool.dma_start(dst, y[:, j % 2, :]).then_inc(y_moved[j % 2], 16)

            bodies(pool, body)
            for i in range(2):
                pool.wait_ge(y_moved[i], 16 * (1 + NT * NB // 2))

        @block.tensor
        def _(pe):
            def product(dst, pairs):
                for i, (lhsT, rhs) in enumerate(pairs):
                    last = pe.matmul(dst, lhsT, rhs, start=(i == 0), stop=(i == len(pairs) - 1))
                return last

            def qkv(j, part, dst):
                cols = slice(part * EMB, (part + 1) * EMB)
                return product(dst, [(xT_sb[:, j % 2, k, :], wqkv[:, k, cols]) for k in range(KC)])

            def turn_qk(a, j, m, ffn):
                b = T_BANK if j == NB - 1 else TURN_BANKS[m]
                if m == 0:
                    wait(qk_low, pe, a, j)
                if j == NB - 1:
                    wait_qkT(pe, a, *((j, m - 1) if m else (j - 1, 1)))
                elif m == 3:
                    wait_qkT(pe, a, j, 0)
                elif m == 2 and ffn:
                    wait(x1T_kept, pe, a - 1, j + 1)
                elif j:
                    wait_qkT(pe, a, j - 1, 3 if m == 0 else m)
                elif m < 2:
                    wait(oT_kept, pe, a - 1, NB - 1)
                for z in range(2):
                    for h in range(HG):
                        src = qk_split[:, z, HG * m + h, :, :].rearrange("p r d -> p (r d)")
                        last = pe.transpose(bank16[b][:, (z * HG + h) * P:(z * HG + h + 1) * P], src, eye16[:, :])
                done(qk_turned, last)

            def scores(t, a, s, ffn):
                b, g = s // NG, s % NG
                dst = bank32[score_bank(s, ffn)]
                wait_qkT(pe, a, b, g)
                if s == 0:
                    wait(k_carried, pe, a, 0)
                    wait(v_kept, pe, a, NB - 1)
                elif ffn:
                    wait(exp_done, pe, a, 2 * s - 1)
                elif s == 1:
                    wait(rope_read, pe, a, NB - 2)
                else:
                    wait(exp_done, pe, a, 2 * s - 3)
                for h in range(HG):
                    head = HG * g + h
                    k_block = qkT[:, 2 * NB - 1 - b, head, :]
                    k_first = free_view(k_block, [[HEADS * P + WINDOW, 2], [1, WINDOW]])
                    for half, keys in ((0, k_first), (1, k_block)):
                        rows = slice(half * WINDOW, (half + 1) * WINDOW)
                        last = pe.matmul(dst[rows, h * P:(h + 1) * P], qkT[:, b, head, rows], keys,
                                         start=True, stop=True)
                done(scores_done, last)

            def turn_probs(a, s, ffn):
                if s == 0:
                    wait_qkT(pe, a, NB - 2, 3)
                else:
                    wait(probsT_kept, pe, a, s - 1)
                for h in range(HG):
                    if h % 2 == 0:
                        wait(exp_done, pe, a, 2 * s + h // 2)
                    last = pe.transpose(bank32[PT_BANK][:, h * P:(h + 1) * P], probs_place(s, ffn)[:, h, :], eye32[:, :])
                done(probs_turned, last)

            def weigh_v(a, s):
                b, g = s // NG, s % NG
                wait(probsT_kept, pe, a, s)
                if g == 0 and b > 0:
                    wait(o_kept, pe, a, b - 1)
                if s == 0:
                    wait_qkT(pe, a, NB - 2, 2)
                for h in range(HG):
                    cols = slice((HG * g + h) * HEAD_DIM, (HG * g + h + 1) * HEAD_DIM)
                    for half, v in ((0, v_cross), (1, v_own)):
                        rows = slice(half * WINDOW, (half + 1) * WINDOW)
                        last = pe.matmul(bank32[O_BANK][rows, cols], probsT[:, h, rows], v[:, b, cols],
                                         start=True, stop=True)
                done(pv_done, last)

            def inner(w, s, dst, chunks=range(KC)):
                cols = slice(s * P, (s + 1) * P)
                for k in chunks:
                    for z in range(2):
                        last = pe.matmul(dst, w[:, k, cols], x1T[:, z, k, :], start=(k == 0 and z == 0),
                                         stop=(k == KC - 1 and z == 1))
                return last

            def turn_o(a, j):
                wait(o_kept, pe, a, j)
                if j == 0:
                    wait(probsT_kept, pe, a, STEPS - 1)
                elif j == 1:
                    wait_qkT(pe, a, NB - 1, NG - 1)
                else:
                    wait(oT_kept, pe, a, j - 2)
                for k in range(KC):
                    last = pe.transpose(bank32[PT_BANK + j % 2][:, k * P:(k + 1) * P],
                                        v_own[:, j, k * P:(k + 1) * P], eye32[:, :])
                done(o_turned, last)

            def body(t, attn, ffn):
                a, f = t, t - 1
                for j in range(NB):
                    if attn:
                        pe.wait_ge(xT_in[j % 2], (a * (NB // 2) + (j // 2 + 1)) * 16)
                        if j == 0:
                            wait(exp_done, pe, a - 1, 2 * STEPS - 1)
                        else:
                            wait(v_kept, pe, a, j - 1)
                        if j == 0 and not ffn:
                            pe.wait_ge(wqkv_in[2], 16)
                        done(v_done, qkv(j, 2, bank32[S_BANK]))
                    if ffn:
                        wait(x1_low, pe, f, j)
                        if j == 0:
                            wait(o_kept, pe, f, NB - 1)
                        elif not attn:
                            wait(x1T_kept, pe, f, j - 2)
                        elif j == 1:
                            wait(x1T_kept, pe, f, 0)
                        else:
                            wait_qkT(pe, a, j - 2, 2)
                        for z in range(2):
                            for k in range(KC):
                                c = (z * KC + k) * P
                                last = pe.transpose(bank16[x1_bank(j, attn)][:, c:c + P],
                                                    x1_split[:, j, z, k * P:(k + 1) * P], eye16[:, :])
                        done(x1_turned, last)
                    if attn:
                        if j < 2:
                            wait(proj_read, pe, a - 1, NB - 1)
                        else:
                            wait(rope_read, pe, a, j - 2)
                        for part in range(2):
                            if j == 0 and not ffn:
                                pe.wait_ge(wqkv_in[part], 16)
                            last = qkv(j, part, bank32[2 * (j % 2) + part])
                        done(qk_done, last)
                        if j == 1 and not ffn:
                            pe.wait_ge(consts_ready, 1)
                        if j:
                            for m in range(NG):
                                turn_qk(a, j - 1, m, ffn)
                if attn and not ffn:
                    scores(t, a, 0, ffn)
                for s in range(STEPS):
                    gate_bank, up_bank = bank32[2 * (s % 2)], bank32[2 * (s % 2) + 1]
                    if attn:
                        if ffn:
                            scores(t, a, s, ffn)
                        elif s + 1 < STEPS:
                            scores(t, a, s + 1, ffn)
                        if s and not ffn:
                            weigh_v(a, s - 1)
                    if ffn:
                        if s == 0:
                            wait(x1T_kept, pe, f, NB - 1)
                        if s >= 2:
                            wait(gated, pe, f, s - 2)
                        elif attn:
                            wait(rope_read, pe, a, NB - 2 + s)
                        else:
                            wait(proj_read, pe, a - 1, NB - 1)
                        done(gate_done, inner(wg, s, gate_bank))
                        if attn and s:
                            weigh_v(a, s - 1)
                        if s >= 2:
                            wait(fused, pe, f, s - 2)
                        done(up_done, inner(wu, s, up_bank))
                    if attn:
                        turn_probs(a, s, ffn)
                    if attn and TURN_AT <= s < TURN_AT + NG:
                        turn_qk(a, NB - 1, s - TURN_AT, ffn)
                if attn:
                    weigh_v(a, STEPS - 1)
                if attn:
                    turn_o(a, 0)
                for j in range(NB):
                    if attn and j + 1 < NB:
                        turn_o(a, j + 1)
                    if ffn:
                        if j < 2:
                            wait(fuse_low, pe, f, STEPS - 2)
                        else:
                            wait(down_read, pe, f, j - 2)
                        rows = slice(j * P, (j + 1) * P)
                        for s in range(STEPS):
                            if j == 0 and s == STEPS - 1:
                                wait(fuse_low, pe, f, STEPS - 1)
                            for z in range(2):
                                last = pe.matmul(bank32[j % 2], fuse[:, s, z, rows], wd[:, s, :],
                                                 start=(s == 0 and z == 0), stop=(s == STEPS - 1 and z == 1))
                        done(down_done, last)
                    if attn:
                        if j == 0 and not ffn:
                            pe.wait_ge(wout_in, 16)
                        wait(oT_kept, pe, a, j)
                        if j < 2:
                            if ffn:
                                wait(fused, pe, f, STEPS - 1)
                            else:
                                wait(rope_read, pe, a, NB - 1)
                        else:
                            wait(proj_read, pe, a, j - 2)
                        done(proj_done, product(bank32[2 + j % 2],
                                                 [(oT[:, j % 2, k, :], wout[:, k, :]) for k in range(KC)]))

            body(0, True, False)
            pe.wait_ge(wffn_in, 3 * 16)
            with pe.Fori(1, NT) as t:
                body(t, True, True)
            body(NT, False, True)

        @block.scalar
        def _(act):
            def copy(dst, src, scale=1.0):
                return act.activation(dst, src, ACT.Copy, scale=scale)

            def keep_fuse_high(f, s):
                wait(fused, act, f, s)
                done(fuse_high, copy(fuse[:, s, 0, :], ffn_tmp[:, s % 2, :]))

            def keep_oT(a, j):
                wait(o_turned, act, a, j)
                wait(proj_done, act, a, j - 2)
                done(oT_kept, copy(oT[:, j % 2, :, :].rearrange("p k c -> p (k c)"), bank32[PT_BANK + j % 2]))

            def gate_tanh(f, s):
                wait(gate_done, act, f, s)
                if s >= 2:
                    wait(fuse_low, act, f, s - 2)
                done(tanh_done, act.activation(ffn_tmp[:, s % 2, :], bank32[2 * (s % 2)], ACT.Tanh,
                                                scale=tanh_scale[:, s:s + 1]))

            def split_high(a, j, parts=range(4)):
                wait(rope_done, act, a, j)
                wait(qk_turned, act, a, NG * j - 1)
                for i in parts:
                    z, odd = i // 2, i % 2
                    src = free_view(rope_t[2 * odd], [[HALF, HEADS], [0, 2], [1, HALF]], z * EMB // 2)
                    twice = slice(0, 2) if z == 0 else slice(0, 4, 2)
                    done(qk_high, copy(qk_split[:, z, :, twice, odd * HALF:(odd + 1) * HALF], src))

            def body(t, attn, ffn):
                a, f = t, t - 1
                for j in range(NB):
                    if attn:
                        if ffn:
                            wait(o_turned, act, a - 1, j)
                        if j == 0 and ffn:
                            wait(v_kept, act, a - 1, NB - 1)
                            copy(v_cross[WINDOW:P, 0, :], v_cross[WINDOW:P, NB, :])
                        wait(v_done, act, a, j)
                        copy(v_own[:, j, :], bank32[S_BANK])
                        copy(v_cross[0:WINDOW, j, :], bank32[S_BANK][0:WINDOW, :])
                        done(v_kept, copy(v_cross[WINDOW:P, j + 1, :], bank32[S_BANK][WINDOW:P, :]))
                    if ffn:
                        wait(x1_turned, act, f, j)
                        if j == 0:
                            wait(proj_read, act, f, NB - 1)
                        done(x1T_kept, copy(x1T[:, :, :, j * P:(j + 1) * P],
                                             bank16[x1_bank(j, attn)].rearrange("p (z k c) -> p z k c", z=2, k=KC)))
                    if attn:
                        if j:
                            for m in (1, 3):
                                wait(qk_turned, act, a, NG * (j - 1) + m)
                                done(qkT_kept_s, copy(*turned_qk(j - 1, m)))
                        if j < NB - 1:
                            split_high(a, j)
                for s in range(STEPS):
                    b, g = s // NG, s % NG
                    if ffn and s:
                        keep_fuse_high(f, s - 1)
                    if ffn and s:
                        gate_tanh(f, s)
                    if attn:
                        wait(bias_done, act, a, s)
                        wait(probs_turned, act, a, s - 1 if ffn else s - 2)
                        if g == 0:
                            wait(o_kept, act, a, b - 2)
                        for h in range(HG):
                            src = bank32[score_bank(s, ffn)][:, h * P:(h + 1) * P]
                            last = act.activation(probs_place(s, ffn)[:, h, :], src, ACT.Exp,
                                                  bias=neg_max[:, s % 2, h:h + 1], scale=scales[:, 10:11],
                                                  accum_out=row_sum[:, b % 2, HG * g + h:HG * g + h + 1])
                            if h % 2:
                                done(exp_done, last)
                    if ffn and not s:
                        gate_tanh(f, s)
                    if attn:
                        wait(probs_turned, act, a, s)
                        wait(pv_done, act, a, s - 1)
                        done(probsT_kept, copy(probsT[:, :, :].rearrange("p h c -> p (h c)"), bank32[PT_BANK]))
                        if 0 <= s - (SPLIT_FROM - 1) < 4:
                            split_high(a, NB - 1, [s - (SPLIT_FROM - 1)])
                if ffn:
                    keep_fuse_high(f, STEPS - 1)
                if attn:
                    keep_oT(a, 0)
                    for j in range(NB):
                        if j + 1 < NB:
                            keep_oT(a, j + 1)
                        wait(x1_ready, act, a, j)
                        done(x1_high, copy(x1_split[:, j, 0, :], x1[:, j, :], X1_SCALE))

            act.wait_ge(consts_ready, 1)
            bodies(act, body)

        @block.vector
        def _(dve):
            def keep_qkT(a, j, m):
                wait(qk_turned, dve, a, NG * j + m)
                done(qkT_kept_v, dve.tensor_copy(*turned_qk(j, m)))

            def rope_products(a, j):
                even, odd = bank32[2 * (j % 2)], bank32[2 * (j % 2) + 1]
                heads = [[HALF, 2 * HEADS], [1, HALF]]

                def table(i):
                    return free_view(tables[:, j, i, :], [[0, 2 * HEADS], [1, HALF]])

                wait(qk_done, dve, a, j)
                wait(qk_high, dve, a, 4 * j - 1)
                for i, src in enumerate((even, odd, odd, even)):
                    last = dve.tensor_tensor(free_view(rope_t[i], heads), free_view(src, heads), table(i), ALU.mult)
                done(rope_read, last)

            def rope_sums(a, j):
                wait(rope_read, dve, a, j)
                dve.tensor_tensor(rope_t[0], rope_t[0], rope_t[1], ALU.subtract)
                done(rope_done, dve.tensor_tensor(rope_t[2], rope_t[2], rope_t[3], ALU.add))

            def split_low(a, j, parts=range(4)):
                for i in parts:
                    z, odd = i // 2, i % 2
                    wait(qk_high, dve, a, 4 * j + i)
                    part = slice(odd * HALF, (odd + 1) * HALF)
                    src = free_view(rope_t[2 * odd], [[HALF, HEADS], [0, 2], [1, HALF]], z * EMB // 2)
                    high = free_view(qk_split[:, z, 0, 0, part], [[P, HEADS], [0, 2], [1, HALF]])
                    twice = slice(2, 4) if z == 0 else slice(1, 4, 2)
                    last = dve.tensor_tensor(qk_split[:, z, :, twice, part], src, high, ALU.subtract)
                if parts[-1] == 3:
                    done(qk_low, last)

            def normalise_o(a, b):
                wait(pv_done, dve, a, NG * (b + 1) - 1)
                done(sum_inverted, dve.reciprocal(inv_sum[:, :], row_sum[:, b % 2, :]))
                wait(sum_inverted, dve, a, b)
                view = [[HEAD_DIM, HEADS], [1, HEAD_DIM]]
                done(o_kept, dve.tensor_tensor(free_view(v_own[:, b, :], view), free_view(bank32[O_BANK], view),
                                                free_view(inv_sum[:, :], [[1, HEADS], [0, HEAD_DIM]]), ALU.mult))

            def keep_fuse_low(f, s):
                wait(fuse_high, dve, f, s)
                done(fuse_low, dve.tensor_tensor(fuse[:, s, 1, :], ffn_tmp[:, s % 2, :], fuse[:, s, 0, :],
                                                  ALU.subtract))

            def moments(chain, tile, first, rows, z):
                st, mv = stats[:, z, :], mean_var[:, z, :]
                done(chain, dve.bn_stats(st, rows))
                wait(chain, dve, tile, first)
                dve.tensor_tensor(mv[:, 0:2], st[:, 1:3], st[:, 4:6], ALU.add)
                done(chain, dve.tensor_tensor(mv[:, 2:3], st[:, 1:2], st[:, 4:5], ALU.subtract))
                wait(chain, dve, tile, first + 1)
                dve.tensor_scalar(mv[:, 0:1], mv[:, 0:1], 0.5, None, ALU.mult)
                dve.scalar_tensor_tensor(out=mv[:, 3:4], in0=mv[:, 2:3], scalar=0.25, in1=mv[:, 2:3],
                                         op0=ALU.mult, op1=ALU.mult)
                done(chain, dve.tensor_scalar(mv[:, 1:2], mv[:, 1:2], 1.0 / EMB, EPS, ALU.mult, ALU.add))
                wait(chain, dve, tile, first + 2)
                done(chain, dve.tensor_tensor(mv[:, 1:2], mv[:, 1:2], mv[:, 3:4], ALU.add))

            def body(t, attn, ffn):
                a, f = t, t - 1
                if attn:
                    before = qkT[:, 2 * NB, :, WINDOW:P]
                    if ffn:
                        wait_qkT(dve, a - 1, NB - 1, NG - 1)
                        done(k_carried, dve.tensor_copy(before, qkT[:, NB, :, WINDOW:P]))
                    else:
                        done(k_carried, dve.memset(before, 0.0))
                    dve.wait_ge(tables_in, (a + 1) * 16)
                    flat = tables[:, :, :, :].rearrange("p b c i -> p (b c i)")
                    done(tables_scaled, dve.tensor_scalar(flat, flat, scales[:, 9:10], None, ALU.mult))
                    wait(tables_scaled, dve, a, 0)
                    for j in range(NB):
                        if j:
                            keep_qkT(a, j - 1, 0)
                            keep_qkT(a, j - 1, 2)
                        if j < NB - 1:
                            rope_products(a, j)
                            rope_sums(a, j)
                            split_low(a, j)
                for s in range(STEPS):
                    if attn:
                        wait(scores_done, dve, a, s)
                        dve.memset(scales[:, 3:4], 0.0)
                        mask = mask_start if (isinstance(t, int) and t == 0 and s < NG) else mask_tile
                        for h in range(HG):
                            unit = bank32[score_bank(s, ffn)][:, h * P:(h + 1) * P]
                            last = dve.tensor_tensor_reduce(out=unit, in0=unit, in1=mask[:, :], scale=1.0, scalar=MASKED,
                                                            op0=ALU.add, op1=ALU.max,
                                                            accum_out=row_max[:, s % 2, h:h + 1])
                        done(max_done, last)
                        wait(max_done, dve, a, s)
                        done(bias_done, dve.tensor_scalar(neg_max[:, s % 2, :], row_max[:, s % 2, :],
                                                           scales[:, 11:12], None, ALU.mult))
                        if s == 0:
                            rope_products(a, NB - 1)
                        if s == 1:
                            rope_sums(a, NB - 1)
                    if ffn and s:
                        keep_fuse_low(f, s - 1)
                    if attn and s and s % NG == 0:
                        normalise_o(a, s // NG - 1)
                    if ffn:
                        tmp = ffn_tmp[:, s % 2, :]
                        wait(tanh_done, dve, f, s)
                        done(gated, dve.scalar_tensor_tensor(out=tmp, in0=tmp, scalar=1.0, in1=bank32[2 * (s % 2)],
                                                              op0=ALU.add, op1=ALU.mult))
                        wait(up_done, dve, f, s)
                        wait(gated, dve, f, s)
                        done(fused, dve.scalar_tensor_tensor(out=tmp, in0=bank32[2 * (s % 2) + 1],
                                                              scalar=fuse_scale[:, s:s + 1], in1=tmp,
                                                              op0=ALU.mult, op1=ALU.mult))
                    if attn and 0 <= s - SPLIT_FROM < 4:
                        split_low(a, NB - 1, [s - SPLIT_FROM])
                    if attn and TURN_AT <= s < TURN_AT + NG:
                        keep_qkT(a, NB - 1, s - TURN_AT)
                if attn:
                    normalise_o(a, NB - 1)
                if ffn:
                    keep_fuse_low(f, STEPS - 1)
                for j in range(NB):
                    rows_y, rows_x1 = y[:, j % 2, :], x1[:, j, :]
                    if ffn:
                        wait(down_done, dve, f, j)
                        dve.wait_ge(y_moved[j % 2], (f * (NB // 2) + (j // 2 + 1)) * 16)
                        done(down_read, dve.tensor_tensor(rows_y, bank32[j % 2], sdown[:, :], ALU.mult))
                        wait(down_read, dve, f, j)
                        done(ln2_chain, dve.tensor_tensor(rows_y, rows_y, rows_x1, ALU.add))
                        wait(ln2_chain, dve, f, 5 * j)
                        moments(ln2_chain, f, 5 * j + 1, rows_y, 1)
                    if attn:
                        if j == 0:
                            dve.wait_ge(rows_in, (a + 1) * 16)
                        wait(proj_done, dve, a, j)
                        done(proj_read, dve.tensor_tensor(rows_x1, bank32[2 + j % 2], x_rows[:, j, :], ALU.add))
                        wait(proj_read, dve, a, j)
                        moments(ln1_chain, a, 4 * j, rows_x1, 0)
                    if ffn:
                        wait(rstd2, dve, f, j)
                        done(y_ready, dve.tensor_scalar(rows_y, rows_y, mean_var[:, 1, 0:1], rstd[:, 1:2],
                                                         ALU.subtract, ALU.mult))
                    if attn:
                        wait(rstd1, dve, a, j)
                        done(x1_ready, dve.tensor_scalar(rows_x1, rows_x1, mean_var[:, 0, 0:1], rstd[:, 0:1],
                                                          ALU.subtract, ALU.mult))
                        wait(x1_high, dve, a, j)
                        done(x1_low, dve.scalar_tensor_tensor(out=x1_split[:, j, 1, :], in0=rows_x1, scalar=X1_SCALE,
                                                               in1=x1_split[:, j, 0, :], op0=ALU.mult,
                                                               op1=ALU.subtract))

            dve.memset(v_cross[WINDOW:P, 0, :], 0.0)
            dve.wait_ge(const_in, 3 * 16)
            for i in range(2):
                dve.wait_ge(y_moved[i], 16)
            dve.tensor_copy(eye32[:, :], raw_const[:, 0:P])
            dve.tensor_copy(eye16[:, :], raw_const[:, 0:P])
            dve.tensor_copy(mask_tile[:, :], raw_const[:, P:2 * P])
            dve.tensor_copy(mask_start[:, :], raw_const[:, 2 * P:3 * P])
            dve.tensor_scalar(tanh_scale[:, :], s_raw[:, 0:STEPS], 0.5 / X1_SCALE, None, ALU.mult)
            dve.tensor_tensor(fuse_scale[:, :], s_raw[:, 0:STEPS], s_raw[:, STEPS:2 * STEPS], ALU.mult)\
                .then_inc(consts_ready, 1)
            dve.wait_ge(consts_ready, 1)
            dve.tensor_reduce(scales[:, 2:3], fuse_scale[:, :], AX.X, ALU.max,
                              apply_absolute_value=True).then_inc(setup, 1)
            for part in range(2):
                dve.wait_ge(wqkv_in[part], 16)
                dve.tensor_reduce(scales[:, 7 + part:8 + part], wqkv[:, :, part * EMB:(part + 1) * EMB], AX.XY, ALU.max,
                                  apply_absolute_value=True).then_inc(setup, 1)
            for c in range(NCH):
                dve.wait_ge(chunk_in[c], 16)
                dve.tensor_reduce(chunk_max[:, c:c + 1], stage[c], AX.X, ALU.max,
                                  apply_absolute_value=True).then_inc(setup, 1)
            dve.wait_ge(setup, NCH + 3)
            dve.tensor_tensor(scales[:, 1:2], scales[:, 7:8], scales[:, 8:9], ALU.max)
            dve.tensor_reduce(scales[:, 0:1], chunk_max[:, :], AX.X, ALU.max).then_inc(setup, 1)
            dve.wait_ge(pool_setup, 2)
            count = [NCH + 4]

            def chained(instruction):
                count[0] += 1
                instruction.then_inc(setup, 1)
                dve.wait_ge(setup, count[0])

            big = scales[:, 4:7]
            chained(dve.tensor_scalar(big, big, 1e-12, None, ALU.max))
            chained(dve.tensor_scalar(big.bitcast(I32), big.bitcast(I32), EXPONENT_BITS, None, ALU.bitwise_and))
            chained(dve.tensor_tensor(scales[:, 7:8], scales[:, 4:5], scales[:, 5:6], ALU.mult))
            chained(dve.tensor_scalar(scales[:, 7:8], scales[:, 7:8], 0.125, None, ALU.mult))
            chained(dve.reciprocal(scales[:, 9:10], scales[:, 7:8]))
            chained(dve.tensor_scalar(scales[:, 10:11], scales[:, 7:8], scales[:, 7:8], SCALE, ALU.mult, ALU.mult))
            chained(dve.tensor_scalar(scales[:, 11:12], scales[:, 10:11], -1.0, None, ALU.mult))
            chained(dve.reciprocal(scales[:, 8:9], scales[:, 6:7]))
            chained(dve.tensor_scalar(fuse_scale[:, :], fuse_scale[:, :], scales[:, 8:9],
                                      0.5 * 2.0 ** -18 / X1_SCALE ** 2, ALU.mult, ALU.mult))
            dve.wait_ge(sdown_in, 16)
            chained(dve.tensor_scalar(sdown[:, :], sdown[:, :], scales[:, 6:7], 2.0 ** 18, ALU.mult, ALU.mult))
            bodies(dve, body)


_OUT = (1, 4096, 512)


def kernel(L0_attn_x, L0_attn_w_qkv, L0_attn_w_out, L0_attn_w_c1, L0_attn_w_c2, L0_ffn_w_gate, L0_ffn_w_up,
           L0_ffn_w_down, L0_ffn_s_gate, L0_ffn_s_up, L0_ffn_s_down):
    import numpy as np
    import concourse.bacc as bacc
    from concourse.bass_utils import run_bass_kernel_spmd

    x = np.asarray(L0_attn_x)[0]
    n_rows = x.shape[0]
    w = np.asarray(L0_attn_w_qkv)
    q, k, v = w[0:EMB], w[EMB:2 * EMB], w[2 * EMB:3 * EMB]
    w_qkvT = np.ascontiguousarray(np.concatenate([q[0::2], k[0::2], q[1::2], k[1::2], v], axis=0).T)

    inv_freq = np.float32(1.0) / np.power(np.float32(10000.0),
                                          np.arange(0, HEAD_DIM, 2, dtype=np.float32) / np.float32(HEAD_DIM))
    freqs = np.outer(np.arange(n_rows, dtype=np.float32), inv_freq.astype(np.float32))
    cos, sin = np.cos(freqs), np.sin(freqs)
    even = np.arange(0, HEAD_DIM, 2) % HALF
    odd = np.arange(1, HEAD_DIM, 2) % HALF
    rope = np.concatenate([cos[:, even], sin[:, even], cos[:, odd], sin[:, odd]], axis=1).astype(np.float32)

    row, key = np.arange(WINDOW)[:, None], np.arange(WINDOW)[None, :]
    own = np.where(key <= row, 0.0, MASKED)
    earlier = np.where(key > row, 0.0, MASKED)
    nothing = np.full((WINDOW, WINDOW), MASKED)
    mask_mid = np.block([[own, earlier], [earlier, own]]).astype(np.float32)
    mask_first = np.block([[own, nothing], [earlier, own]]).astype(np.float32)

    arrays = {
        "x": x,
        "xT": np.ascontiguousarray(x.T),
        "w_qkvT": w_qkvT,
        "w_outT": np.ascontiguousarray(np.asarray(L0_attn_w_out).T),
        "w_gate": np.ascontiguousarray(L0_ffn_w_gate).view(np.int32),
        "w_up": np.ascontiguousarray(L0_ffn_w_up).view(np.int32),
        "w_down": np.ascontiguousarray(L0_ffn_w_down).view(np.int32),
        "s_gate": np.ascontiguousarray(np.asarray(L0_ffn_s_gate).reshape(STEPS, P).T),
        "s_up": np.ascontiguousarray(np.asarray(L0_ffn_s_up).reshape(STEPS, P).T),
        "s_down": np.ascontiguousarray(np.asarray(L0_ffn_s_down).reshape(1, EMB)),
        "rope": rope,
        "mask_mid": mask_mid,
        "mask_first": mask_first,
        "eye": np.eye(P, dtype=np.float32),
    }
    nc = bacc.Bacc("TRN2", target_bir_lowering=False, num_devices=1)
    args = [nc.dram_tensor(n, a.shape, mybir.dt.from_np(a.dtype), kind="ExternalInput").ap()
            for n, a in arrays.items()]
    out = nc.dram_tensor("out", (n_rows, EMB), F32, kind="ExternalOutput").ap()
    build(nc, *args, out)
    result = run_bass_kernel_spmd(nc, [arrays], core_ids=[0])
    return result.results[0]["out"].reshape(_OUT)
```

```python
from contextlib import ExitStack

import concourse.bass as bass
from concourse import mybir

F32 = mybir.dt.float32
F16 = mybir.dt.float16
BF16 = mybir.dt.bfloat16
I32 = mybir.dt.int32
ALU = mybir.AluOpType
ACT = mybir.ActivationFunctionType
AX = mybir.AxisListType

P = 128
EMB = 512
HEADS = 16
HEAD_DIM = EMB // HEADS
HALF = HEAD_DIM // 2
WINDOW = 64
INTER = 2048
EPS = 1e-5
SCALE = float(HEAD_DIM) ** -0.5

KC = EMB // P
TILE = 512
NB = TILE // P
HG = 4
NG = HEADS // HG
STEPS = NB * NG
X1_SCALE = 2.0 ** 10
MASKED = -(2.0 ** 120)
EXPONENT_BITS = 0x7F800000
SPLIT_FROM = 2
SEARCHED = (2, 3, 3)
SEARCH_FROM = 14
TURN_AT = 7
assert STEPS == INTER // P and WINDOW * 2 == P


def done(kind, instruction, steps=1):
    instruction.then_inc(kind[0], steps)


def wait(kind, eng, tile, n):
    sem, per_tile = kind
    value = tile * per_tile + (n + 1)
    if isinstance(value, int) and value <= 0:
        return
    eng.wait_ge(sem, value)


def free_view(ap, dims, offset=0):
    return bass.AP(ap.tensor, ap.offset + offset, [list(ap.ap[0])] + [list(d) for d in dims])


def build(nc, x, xT, w_qkvT, w_outT, w_gate, w_up, w_down, s_gate, s_up, s_down, rope, mask_mid, mask_first,
          eye, out):
    I8 = mybir.dt.int8
    w_gate, w_up, w_down = (w.bitcast(I8) for w in (w_gate, w_up, w_down))
    S = x.shape[0]
    NT = S // TILE
    ctx = ExitStack()
    with ctx:
        def sb(name, shape, dt):
            return ctx.enter_context(nc.sbuf_tensor(name, shape, dt))

        def sem(name):
            return ctx.enter_context(nc.semaphore(name))

        wqkv = sb("wqkv", [P, KC, 3 * EMB], F32)
        wout = sb("wout", [P, KC, EMB], F32)
        wg = sb("wg", [P, KC, INTER], F16)
        wu = sb("wu", [P, KC, INTER], F16)
        wd = sb("wd", [P, STEPS, EMB], F16)
        eye32 = sb("eye32", [P, P], F32)
        eye16 = sb("eye16", [P, P], F16)
        mask_tile = sb("mask_tile", [P, P], BF16)
        mask_start = sb("mask_start", [P, P], BF16)
        sdown = sb("sdown", [P, EMB], F32)
        tanh_scale = sb("tanh_scale", [P, STEPS], F32)
        fuse_scale = sb("fuse_scale", [P, STEPS], F32)
        largest = sb("largest", [P, 4], F32)
        power = sb("power", [P, 4], F32)
        part_max = sb("part_max", [P, 2], F32)
        half_max = sb("half_max", [P, 2 * S // TILE - 1], F32)
        qk_scale = sb("qk_scale", [P, 2, 4], F32)
        carry_scale = sb("carry_scale", [P, 1], F32)
        fuse_inv = sb("fuse_inv", [P, 1], F32)
        wait_taker = sb("wait_taker", [P, 1], F32)
        half_power = sb("half_power", [P, 1], F32)

        xT_sb = sb("xT_sb", [P, 2, KC, P], F32)
        tables = sb("tables", [P, NB, 4, HALF], F32)
        qkT = sb("qkT", [P, 2 * NB + 1, HEADS, P], F16)
        v_own = sb("v_own", [P, NB, EMB], F32)
        v_cross = sb("v_cross", [P, NB + 1, EMB], F32)
        probs = sb("probs", [P, HG, P], F32)
        probsT = sb("probsT", [P, HG, P], F32)
        row_sum = sb("row_sum", [P, 2, HG], F32)
        inv_sum = sb("inv_sum", [P, 2, HG], F32)
        x1 = sb("x1", [P, NB, EMB], F32)
        x1T = sb("x1T", [P, 2, KC, TILE], F16)
        fuse = sb("fuse", [P, STEPS, 2, TILE], F16)
        ffn_tmp = sb("ffn_tmp", [P, 2, TILE], F32)
        y = sb("y", [P, 2, EMB], F32)
        row_max = sb("row_max", [P, 2, HG], F32)
        neg_max = sb("neg_max", [P, 2, HG], F32)
        stats = sb("stats", [P, 2, 6], F32)
        mean_var = sb("mean_var", [P, 2, 4], F32)
        rstd = sb("rstd", [P, 2], F32)

        x_rows = x1T[:, :, :, :].rearrange("p a k t -> p (a k t)").bitcast(F32).rearrange("p (b n) -> p b n", b=NB)
        fuse32 = fuse[:, :, :, :].rearrange("p s a t -> p (s a t)").bitcast(F32)
        ROPE_AT, SPLIT_AT = 8, 12
        rope_t = [fuse32[:, (ROPE_AT + i) * EMB:(ROPE_AT + i + 1) * EMB] for i in range(4)]
        split_at = SPLIT_AT * 2 * TILE
        qk_split = fuse[:, :, :, :].rearrange("p s a t -> p (s a t)")[:, split_at:split_at + 2 * HEADS * P]\
            .rearrange("p (z h r d) -> p z h r d", z=2, h=HEADS, r=4)
        x1_split = qkT[:, 2:4, :, :].rearrange("p s h c -> p (s h c)").rearrange("p (b z n) -> p b z n", b=NB, z=2)

        bank = [ctx.enter_context(nc.psum_tensor(f"bank{i}", [P, 512], F32)) for i in range(8)]
        bank32 = [b[:, :] for b in bank]
        bank16 = [b[:, :].bitcast(F16) for b in bank]
        S_BANK, PT_BANK, T_BANK, O_BANK = 4, 5, 6, 7
        TURN_BANKS = (PT_BANK, T_BANK, O_BANK, PT_BANK)

        def ev(name, per_tile):
            return sem(name), per_tile

        v_done = ev("v_done", NB)
        qk_done = ev("qk_done", NB)
        x1_turned = ev("x1_turned", NB)
        qk_turned = ev("qk_turned", STEPS)
        scores_done = ev("scores_done", STEPS)
        probs_turned = ev("probs_turned", STEPS)
        pv_done = ev("pv_done", STEPS)
        gate_done = ev("gate_done", STEPS)
        up_done = ev("up_done", STEPS)
        down_done = ev("down_done", NB)
        proj_done = ev("proj_done", NB)
        v_kept = ev("v_kept", NB)
        x1T_kept = ev("x1T_kept", NB)
        qk_high = ev("qk_high", 4 * NB)
        fuse_high = ev("fuse_high", STEPS)
        qkT_kept_s = ev("qkT_kept_s", 2 * (NB - 1))
        exp_done = ev("exp_done", 2 * STEPS)
        tanh_done = ev("tanh_done", STEPS)
        probsT_kept = ev("probsT_kept", STEPS)
        x1_high = ev("x1_high", NB)
        o_kept = ev("o_kept", NB)
        k_carried = ev("k_carried", 1)
        tables_scaled = ev("tables_scaled", 1)
        even_read = ev("even_read", 1)
        rope_read = ev("rope_read", NB)
        rope_done = ev("rope_done", NB)
        qk_low = ev("qk_low", NB)
        qkT_kept_v = ev("qkT_kept_v", 2 * (NB - 1) + NG)
        max_done = ev("max_done", STEPS)
        bias_done = ev("bias_done", STEPS)
        gated = ev("gated", STEPS)
        fused = ev("fused", STEPS)
        fuse_low = ev("fuse_low", STEPS)
        sum_inverted = ev("sum_inverted", 2 * STEPS)
        probs_ready = ev("probs_ready", 2 * STEPS)
        down_read = ev("down_read", NB)
        ln2_chain = ev("ln2_chain", 5 * NB)
        y_ready = ev("y_ready", NB)
        proj_read = ev("proj_read", NB)
        ln1_chain = ev("ln1_chain", 4 * NB)
        x1_ready = ev("x1_ready", NB)
        x1_low = ev("x1_low", NB)
        rstd2 = ev("rstd2", NB)
        rstd1 = ev("rstd1", NB)
        xT_in = [sem(f"xT_in{i}") for i in range(2)]
        tables_in = sem("tables_in")
        rows_in = sem("rows_in")
        y_moved = [sem(f"y_moved{i}") for i in range(2)]
        wout_in, wffn_in, const_in, sdown_in = sem("wout_in"), sem("wffn_in"), sem("const_in"), sem("sdown_in")
        wqkv_in = [sem(f"wqkv_in{i}") for i in range(3)]
        setup = sem("setup")
        SETUP_MAXIMA, SETUP_ALL = 5, 24
        pool_setup = sem("pool_setup")
        consts_ready = sem("consts_ready")

        wg32, wu32 = (w[:, :, :].rearrange("p k n -> p (k n)").bitcast(F32) for w in (wg, wu))
        x1_flat = x1[:, :, :].rearrange("p b n -> p (b n)")
        PART = NB * EMB
        stage = [x1_flat, wg32[:, 0:PART], wg32[:, PART:2 * PART], wu32[:, 0:PART], wu32[:, PART:2 * PART],
                 fuse32[:, 0:PART], fuse32[:, PART:2 * PART]]
        assert len(stage) == NT - 1 and 2 * PART <= ROPE_AT * EMB
        stage_in = [sem(f"stage_in{i}") for i in range(NT - 1)]
        halves_searched = sem("halves_searched")
        HALVES = 2 * (NT - 1)
        AT_END = sum(SEARCHED) + STEPS - SEARCH_FROM
        assert AT_END <= HALVES
        raw_const = y[:, :, :].rearrange("p a n -> p (a n)")
        s_raw = ffn_tmp[:, 0, 0:2 * STEPS]

        def tile_rows(a):
            return x[bass.ds(a * TILE, TILE), :].rearrange("(b p) n -> p b n", p=P)

        def wait_qkT(eng, a, j, m):
            if j == NB - 1:
                wait(qkT_kept_v, eng, a, 2 * j + m)
            else:
                wait(qkT_kept_s if m % 2 else qkT_kept_v, eng, a, 2 * j + m // 2)

        def turned_qk(j, m):
            b = T_BANK if j == NB - 1 else TURN_BANKS[m]
            q_slot, k_slot = j, 2 * NB - 1 - j
            dst = free_view(qkT[:, q_slot, HG * m, :], [[(k_slot - q_slot) * HEADS * P, 2], [1, HG * P]])
            return dst, bank16[b].rearrange("p (z c) -> p z c", z=2)

        def probs_place(s, ffn):
            return probs[:, :, :] if ffn or s % 2 == 0 else ffn_tmp[:, 1, :].rearrange("p (h c) -> p h c", h=HG)

        def pt_bank(s, ffn):
            return PT_BANK if ffn or s % 2 == 0 else 1

        def probsT_place(s, ffn):
            return probsT[:, :, :] if ffn or s % 2 == 0 else ffn_tmp[:, 0, :].rearrange("p (h c) -> p h c", h=HG)

        def proj_bank(j, ffn):
            return 2 + j % 2 if ffn or j < 2 else j - 2

        def x1_bank(j, attn):
            return O_BANK if attn else (O_BANK, T_BANK, S_BANK, PT_BANK)[j]

        def score_bank(s, ffn):
            return S_BANK if ffn or s % 2 == 0 else 0

        def bodies(eng, body):
            body(0, True, False)
            with eng.Fori(1, NT) as t:
                body(t, True, True)
            body(NT, False, True)

        block = ctx.enter_context(nc.Block())

        @block.sync
        def _(sp):
            def load_xT(a, j):
                wait(qk_done, sp, a, j - 2)
                src = xT.rearrange("(k p) s -> p k s", p=P)[:, :, bass.ds(a * TILE + j * P, P)]
                sp.dma_start(xT_sb[:, j % 2, :, :], src).then_inc(xT_in[j % 2], 16)

            def load_wqkv(part):
                cols = slice(part * EMB, (part + 1) * EMB)
                sp.dma_start(wqkv[:, :, cols], w_qkvT.rearrange("(k p) n -> p k n", p=P)[:, :, cols])\
                    .then_inc(wqkv_in[part], 16)

            def load_stage(which):
                for i in which:
                    dst = stage[i].rearrange("p (b n) -> p b n", b=NB)
                    sp.dma_start(dst, tile_rows(i + 1)).then_inc(stage_in[i], 16)

            load_wqkv(2)

            def body(t, attn, ffn):
                if not attn:
                    return
                a = t
                load_xT(a, 0)
                if not ffn:
                    for src, dst in ((s_gate, s_raw[:, 0:STEPS]), (s_up, s_raw[:, STEPS:2 * STEPS]),
                                     (mask_first, raw_const[:, 2 * P:3 * P])):
                        sp.dma_start(dst, src).then_inc(const_in, 16)
                    load_wqkv(0)
                    sp.dma_start(x_rows, tile_rows(0)).then_inc(rows_in, 16)
                    load_wqkv(1)
                load_xT(a, 1)
                if ffn:
                    wait(rope_read, sp, a - 1, NB - 1)
                src = rope[bass.ds(a * TILE, TILE), :].rearrange("(b p) c -> p b c", p=P)
                sp.dma_start(tables[:, :, :, :].rearrange("p b c i -> p b (c i)"), src).then_inc(tables_in, 16)
                if not ffn:
                    load_stage(range(0, 3))
                load_xT(a, 2)
                if not ffn:
                    load_stage(range(3, 5))
                load_xT(a, 3)
                if ffn:
                    wait(up_done, sp, t - 1, STEPS - 1)
                    sp.dma_start(x_rows, tile_rows(a)).then_inc(rows_in, 16)
                else:
                    load_stage(range(5, NT - 1))
                    sp.dma_start(wout[:, :, :], w_outT.rearrange("(k p) n -> p k n", p=P)).then_inc(wout_in, 16)
                    sp.dma_start(sdown[:, :], s_down.to_broadcast([P, EMB])).then_inc(sdown_in, 16)

            bodies(sp, body)

        @block.gpsimd
        def _(pool):
            pool.memset(half_power[:, :], -0.5).then_inc(pool_setup, 1)
            pool.wait_ge(setup, SETUP_MAXIMA)
            pool.partition_all_reduce(power[:, 0:3], largest[:, 0:3], P, bass.bass_isa.ReduceOp.absmax)\
                .then_inc(pool_setup, 1)
            pool.dma_start(wd[:, :, :], w_down.rearrange("(s p) n -> p s n", p=P)).then_inc(wffn_in, 16)
            pool.wait_ge(halves_searched, HALVES + 1)
            pool.partition_all_reduce(power[:, 3:4], largest[:, 3:4], P, bass.bass_isa.ReduceOp.absmax)\
                .then_inc(pool_setup, 1)
            pool.wait_ge(pool_setup, 3)
            pool.dma_start(wg[:, :, :], w_gate.rearrange("(k p) n -> p k n", p=P)).then_inc(wffn_in, 16)
            pool.dma_start(wu[:, :, :], w_up.rearrange("(k p) n -> p k n", p=P)).then_inc(wffn_in, 16)

            def body(t, attn, ffn):
                if ffn:
                    for s in range(STEPS):
                        wait(fuse_high, pool, t - 1, s)
                        done(fuse_low, pool.tensor_tensor(fuse[:, s, 1, :], ffn_tmp[:, s % 2, :], fuse[:, s, 0, :],
                                                          ALU.subtract))
                for j in range(NB):
                    if ffn:
                        wait(ln2_chain, pool, t - 1, 5 * j + 4)
                        done(rstd2, pool.tensor_tensor(rstd[:, 1:2], mean_var[:, 1, 1:2], half_power[:, :], ALU.pow))
                    if attn:
                        wait(ln1_chain, pool, t, 4 * j + 3)
                        done(rstd1, pool.tensor_tensor(rstd[:, 0:1], mean_var[:, 0, 1:2], half_power[:, :], ALU.pow))

            bodies(pool, body)

        @block.tensor
        def _(pe):
            def product(dst, pairs):
                for i, (lhsT, rhs) in enumerate(pairs):
                    last = pe.matmul(dst, lhsT, rhs, start=(i == 0), stop=(i == len(pairs) - 1))
                return last

            def qkv(j, part, dst):
                cols = slice(part * EMB, (part + 1) * EMB)
                return product(dst, [(xT_sb[:, j % 2, k, :], wqkv[:, k, cols]) for k in range(KC)])

            def turn_qk(a, j, m, ffn):
                b = T_BANK if j == NB - 1 else TURN_BANKS[m]
                if m == 0:
                    wait(qk_low, pe, a, j)
                if j == NB - 1:
                    wait_qkT(pe, a, *((j, m - 1) if m else (j - 1, 1)))
                elif m == 3:
                    wait_qkT(pe, a, j, 0)
                elif m == 2 and ffn:
                    wait(x1T_kept, pe, a - 1, j + 1)
                elif j:
                    wait_qkT(pe, a, j - 1, 3 if m == 0 else m)
                elif m == 0:
                    wait(probsT_kept, pe, a - 1, STEPS - 1)
                elif m == 1:
                    wait_qkT(pe, a - 1, NB - 1, NG - 1)
                for z in range(2):
                    for h in range(HG):
                        src = qk_split[:, z, HG * m + h, :, :].rearrange("p r d -> p (r d)")
                        last = pe.transpose(bank16[b][:, (z * HG + h) * P:(z * HG + h + 1) * P], src, eye16[:, :])
                done(qk_turned, last)

            def scores(t, a, s, ffn):
                b, g = s // NG, s % NG
                dst = bank32[score_bank(s, ffn)]
                wait_qkT(pe, a, b, g)
                if s == 0:
                    wait(k_carried, pe, a, 0)
                    wait(v_kept, pe, a, NB - 1)
                elif ffn:
                    wait(exp_done, pe, a, 2 * s - 1)
                elif s == 1:
                    wait(rope_read, pe, a, NB - 2)
                else:
                    wait(exp_done, pe, a, 2 * s - 3)
                for h in range(HG):
                    head = HG * g + h
                    k_block = qkT[:, 2 * NB - 1 - b, head, :]
                    k_first = free_view(k_block, [[HEADS * P + WINDOW, 2], [1, WINDOW]])
                    for half, keys in ((0, k_first), (1, k_block)):
                        rows = slice(half * WINDOW, (half + 1) * WINDOW)
                        last = pe.matmul(dst[rows, h * P:(h + 1) * P], qkT[:, b, head, rows], keys,
                                         start=True, stop=True)
                done(scores_done, last)

            def turn_probs(a, s, ffn):
                if s == 0:
                    wait_qkT(pe, a, NB - 2, 3)
                elif ffn:
                    wait(probsT_kept, pe, a, s - 1)
                elif s == 1:
                    wait(rope_read, pe, a, NB - 2)
                else:
                    wait(probsT_kept, pe, a, s - 2)
                for h in range(HG):
                    if h % 2 == 0:
                        wait(probs_ready, pe, a, 2 * s + h // 2)
                    last = pe.transpose(bank32[pt_bank(s, ffn)][:, h * P:(h + 1) * P], probs_place(s, ffn)[:, h, :],
                                        eye32[:, :])
                done(probs_turned, last)

            def weigh_v(a, s, ffn):
                b, g = s // NG, s % NG
                wait(probsT_kept, pe, a, s)
                if s == 0:
                    wait_qkT(pe, a, NB - 2, 2)
                elif g == 0:
                    wait(o_kept, pe, a, b - 1)
                dst = bank32[O_BANK][:, g * P:(g + 1) * P]
                for half, v in ((0, v_cross), (1, v_own)):
                    for h in range(HG):
                        rows = slice(half * WINDOW, (half + 1) * WINDOW)
                        cols = slice((HG * g + h) * HEAD_DIM, (HG * g + h + 1) * HEAD_DIM)
                        last = pe.matmul(dst[h * HEAD_DIM:(h + 1) * HEAD_DIM, rows], v[:, b, cols],
                                         probsT_place(s, ffn)[:, h, rows], start=True, stop=True)
                done(pv_done, last)

            def inner(w, s, dst, rows=slice(0, TILE)):
                cols = slice(s * P, (s + 1) * P)
                return product(dst[:, rows], [(w[:, k, cols], x1T[:, z, k, rows]) for k in range(KC) for z in range(2)])

            def body(t, attn, ffn):
                a, f = t, t - 1
                for j in range(NB):
                    if attn:
                        pe.wait_ge(xT_in[j % 2], (a * (NB // 2) + (j // 2 + 1)) * 16)
                        if j == 0:
                            wait(exp_done, pe, a - 1, 2 * STEPS - 1)
                        else:
                            wait(v_kept, pe, a, j - 1)
                        if j == 0 and not ffn:
                            pe.wait_ge(wqkv_in[2], 16)
                        done(v_done, qkv(j, 2, bank32[S_BANK]))
                    if ffn:
                        wait(x1_low, pe, f, j)
                        if j == 0:
                            wait(o_kept, pe, f, NB - 1)
                        elif attn and j == 1:
                            wait(x1T_kept, pe, f, 0)
                        elif attn:
                            wait_qkT(pe, a, j - 2, 2)
                        for z in range(2):
                            for k in range(KC):
                                c = (z * KC + k) * P
                                last = pe.transpose(bank16[x1_bank(j, attn)][:, c:c + P],
                                                    x1_split[:, j, z, k * P:(k + 1) * P], eye16[:, :])
                        done(x1_turned, last)
                    if attn:
                        if j < 2:
                            wait(proj_read, pe, a - 1, NB - 1)
                        else:
                            wait(rope_read, pe, a, j - 2)
                        for part in range(2):
                            if j == 0 and not ffn:
                                pe.wait_ge(wqkv_in[part], 16)
                            last = qkv(j, part, bank32[2 * (j % 2) + part])
                        done(qk_done, last)
                        if j == 1 and not ffn:
                            pe.wait_ge(consts_ready, 1)
                        if j:
                            for m in range(NG):
                                turn_qk(a, j - 1, m, ffn)
                if attn and not ffn:
                    scores(t, a, 0, ffn)
                    scores(t, a, 1, ffn)
                for s in range(STEPS):
                    gate_bank, up_bank = bank32[2 * (s % 2)], bank32[2 * (s % 2) + 1]
                    if attn:
                        if ffn:
                            scores(t, a, s, ffn)
                        elif s + 2 < STEPS:
                            scores(t, a, s + 2, ffn)
                    if ffn:
                        rows = slice(0, TILE)
                        if s == 0 and not attn:
                            wait(proj_read, pe, a - 1, NB - 1)
                            wait(x1T_kept, pe, f, 1)
                            rows = slice(TILE // 2, TILE)
                            inner(wg, s, gate_bank, slice(0, TILE // 2))
                        if s == 0:
                            pe.wait_ge(wffn_in, 3 * 16)
                            wait(x1T_kept, pe, f, NB - 1)
                        if s >= 2:
                            wait(gated, pe, f, s - 2)
                        elif attn and s == 0:
                            wait(rope_read, pe, a, NB - 2)
                        elif attn:
                            wait(even_read, pe, a, 0)
                        done(gate_done, inner(wg, s, gate_bank, rows))
                        if attn and s:
                            weigh_v(a, s - 1, ffn)
                        if attn and 0 <= s - TURN_AT < NG:
                            turn_qk(a, NB - 1, s - TURN_AT, ffn)
                        if s >= 2:
                            wait(fused, pe, f, s - 2)
                        elif attn:
                            wait(rope_read, pe, a, NB - 2 + s)
                        done(up_done, inner(wu, s, up_bank))
                    if attn:
                        turn_probs(a, s, ffn)
                        if s and not ffn:
                            weigh_v(a, s - 1, ffn)
                    if attn and not ffn and 0 <= s - TURN_AT < NG:
                        turn_qk(a, NB - 1, s - TURN_AT, ffn)
                if attn and not ffn:
                    weigh_v(a, STEPS - 1, ffn)
                for j in range(NB):
                    if ffn:
                        if j < 2:
                            wait(fused if j else gated, pe, f, STEPS - 2)
                        else:
                            wait(down_read, pe, f, j - 2)
                        rows = slice(j * P, (j + 1) * P)
                        for s in range(STEPS):
                            if j == 0 and (s == 0 or s >= STEPS - 2):
                                wait(fuse_low, pe, f, STEPS - 3 if s == 0 else s)
                            for z in range(2):
                                last = pe.matmul(bank32[j % 2], fuse[:, s, z, rows], wd[:, s, :],
                                                 start=(s == 0 and z == 0), stop=(s == STEPS - 1 and z == 1))
                        done(down_done, last)
                        if attn and j == 0:
                            weigh_v(a, STEPS - 1, ffn)
                    if attn:
                        if j == 0 and not ffn:
                            pe.wait_ge(wout_in, 16)
                        wait(o_kept, pe, a, j)
                        if not ffn:
                            kind, n = ((rope_read, NB - 1), (rope_read, NB - 1), (exp_done, 2 * STEPS - 1),
                                       (probsT_kept, STEPS - 1))[j]
                            wait(kind, pe, a, n)
                        elif j < 2:
                            wait(fused, pe, f, STEPS - 1)
                        else:
                            wait(proj_read, pe, a, j - 2)
                        done(proj_done, product(bank32[proj_bank(j, ffn)],
                                                 [(v_own[:, j, k * P:(k + 1) * P], wout[:, k, :]) for k in range(KC)]))

            body(0, True, False)
            with pe.Fori(1, NT) as t:
                body(t, True, True)
            body(NT, False, True)

        @block.scalar
        def _(act):
            def copy(dst, src, scale=1.0):
                return act.activation(dst, src, ACT.Copy, scale=scale)

            def keep_fuse_high(f, s):
                wait(fused, act, f, s)
                done(fuse_high, copy(fuse[:, s, 0, :], ffn_tmp[:, s % 2, :]))

            def keep_probsT(a, s, ffn):
                wait(probs_turned, act, a, s)
                wait(pv_done, act, a, s - 1 if ffn else s - 2)
                done(probsT_kept, copy(probsT_place(s, ffn).rearrange("p h c -> p (h c)"), bank32[pt_bank(s, ffn)]))

            def keep_o(a, b):
                wait(pv_done, act, a, NG * (b + 1) - 1)
                done(o_kept, copy(v_own[:, b, :], bank32[O_BANK]))

            def gate_tanh(f, s):
                wait(gate_done, act, f, s)
                if s >= 2:
                    wait(fuse_low, act, f, s - 2)
                done(tanh_done, act.activation(ffn_tmp[:, s % 2, :], bank32[2 * (s % 2)], ACT.Tanh,
                                                scale=tanh_scale[:, s:s + 1]))

            def split_high(a, j, parts=range(4)):
                wait(rope_done, act, a, j)
                wait(qk_turned, act, a, NG * j - 1)
                for i in parts:
                    z, odd = i // 2, i % 2
                    src = free_view(rope_t[2 * odd], [[HALF, HEADS], [0, 2], [1, HALF]], z * EMB // 2)
                    twice = slice(0, 2) if z == 0 else slice(0, 4, 2)
                    done(qk_high, copy(qk_split[:, z, :, twice, odd * HALF:(odd + 1) * HALF], src))

            def body(t, attn, ffn):
                a, f = t, t - 1
                for j in range(NB):
                    if attn:
                        if ffn:
                            wait(proj_done, act, a - 1, j)
                        if j == 0 and ffn:
                            wait(v_kept, act, a - 1, NB - 1)
                            copy(v_cross[WINDOW:P, 0, :], v_cross[WINDOW:P, NB, :])
                        wait(v_done, act, a, j)
                        copy(v_own[:, j, :], bank32[S_BANK])
                        copy(v_cross[0:WINDOW, j, :], bank32[S_BANK][0:WINDOW, :])
                        done(v_kept, copy(v_cross[WINDOW:P, j + 1, :], bank32[S_BANK][WINDOW:P, :]))
                    if ffn:
                        wait(x1_turned, act, f, j)
                        if j == 0:
                            wait(proj_read, act, f, NB - 1)
                        done(x1T_kept, copy(x1T[:, :, :, j * P:(j + 1) * P],
                                             bank16[x1_bank(j, attn)].rearrange("p (z k c) -> p z k c", z=2, k=KC)))
                    if attn:
                        if j:
                            for m in (1, 3):
                                wait(qk_turned, act, a, NG * (j - 1) + m)
                                done(qkT_kept_s, copy(*turned_qk(j - 1, m)))
                        if j < NB - 1:
                            split_high(a, j)
                for s in range(STEPS):
                    if attn:
                        wait(bias_done, act, a, s)
                        wait(probs_turned, act, a, s - 1 if ffn else s - 2)
                        for h in range(HG):
                            src = bank32[score_bank(s, ffn)][:, h * P:(h + 1) * P]
                            last = act.activation(probs_place(s, ffn)[:, h, :], src, ACT.Exp,
                                                  bias=neg_max[:, s % 2, h:h + 1], scale=qk_scale[:, int(ffn), 2:3],
                                                  accum_out=row_sum[:, s % 2, h:h + 1])
                            if h % 2:
                                done(exp_done, last)
                    if ffn:
                        gate_tanh(f, s)
                        if s:
                            keep_fuse_high(f, s - 1)
                    if attn and ffn:
                        if s and s % NG == 0:
                            keep_o(a, s // NG - 1)
                        keep_probsT(a, s, ffn)
                    if attn and not ffn:
                        if s:
                            keep_probsT(a, s - 1, ffn)
                        if s > NG and s % NG == 1:
                            keep_o(a, s // NG - 1)
                    if attn and 0 <= s - (SPLIT_FROM - 1) < 4:
                        split_high(a, NB - 1, [s - (SPLIT_FROM - 1)])
                if ffn:
                    keep_fuse_high(f, STEPS - 1)
                if attn:
                    if not ffn:
                        keep_probsT(a, STEPS - 1, ffn)
                    keep_o(a, NB - 1)
                for j in range(NB):
                    if ffn:
                        wait(y_ready, act, f, j)
                        dst = out[bass.ds(f * TILE + j * P, P), :]
                        act.dma_start(dst, y[:, j % 2, :]).then_inc(y_moved[j % 2], 16)
                    if attn:
                        wait(x1_ready, act, a, j)
                        done(x1_high, copy(x1_split[:, j, 0, :], x1[:, j, :], X1_SCALE))

            act.dma_start(raw_const[:, 0:P], eye).then_inc(y_moved[0], 16)
            act.dma_start(raw_const[:, P:2 * P], mask_mid).then_inc(y_moved[1], 16)
            act.wait_ge(consts_ready, 1)
            bodies(act, body)
            for i in range(2):
                act.wait_ge(y_moved[i], 16 * (1 + NT * NB // 2))

        @block.vector
        def _(dve):
            def keep_qkT(a, j, m):
                wait(qk_turned, dve, a, NG * j + m)
                done(qkT_kept_v, dve.tensor_copy(*turned_qk(j, m)))

            def rope_products(a, j, which=(0, 3, 1, 2)):
                even, odd = bank32[2 * (j % 2)], bank32[2 * (j % 2) + 1]
                heads = [[HALF, 2 * HEADS], [1, HALF]]

                def table(i):
                    return free_view(tables[:, j, i, :], [[0, 2 * HEADS], [1, HALF]])

                wait(qk_done, dve, a, j)
                wait(qk_high, dve, a, 4 * j - 1)
                for i in which:
                    src = (even, odd, odd, even)[i]
                    last = dve.tensor_tensor(free_view(rope_t[i], heads), free_view(src, heads), table(i), ALU.mult)
                done(rope_read if which[-1] == 2 else even_read, last)

            def rope_sums(a, j):
                wait(rope_read, dve, a, j)
                dve.tensor_tensor(rope_t[0], rope_t[0], rope_t[1], ALU.subtract)
                done(rope_done, dve.tensor_tensor(rope_t[2], rope_t[2], rope_t[3], ALU.add))

            def split_low(a, j, parts=range(4)):
                for i in parts:
                    z, odd = i // 2, i % 2
                    wait(qk_high, dve, a, 4 * j + i)
                    part = slice(odd * HALF, (odd + 1) * HALF)
                    src = free_view(rope_t[2 * odd], [[HALF, HEADS], [0, 2], [1, HALF]], z * EMB // 2)
                    high = free_view(qk_split[:, z, 0, 0, part], [[P, HEADS], [0, 2], [1, HALF]])
                    twice = slice(2, 4) if z == 0 else slice(1, 4, 2)
                    last = dve.tensor_tensor(qk_split[:, z, :, twice, part], src, high, ALU.subtract)
                if parts[-1] == 3:
                    done(qk_low, last)

            def search(i):
                dve.wait_ge(stage_in[i // 2], 16)
                half = stage[i // 2][:, i % 2 * PART // 2:(i % 2 + 1) * PART // 2]
                dve.tensor_reduce(half_max[:, i + 1:i + 2], half, AX.X, ALU.max,
                                  apply_absolute_value=True).then_inc(halves_searched, 1)

            def invert_sums(a, s, pairs):
                heads = slice(2 * pairs[0], 2 * pairs[-1] + 2)
                wait(exp_done, dve, a, 2 * s + pairs[-1])
                done(sum_inverted, dve.reciprocal(inv_sum[:, s % 2, heads], row_sum[:, s % 2, heads]), len(pairs))

            def weights(a, s, ffn, pairs):
                heads = slice(2 * pairs[0], 2 * pairs[-1] + 2)
                wait(sum_inverted, dve, a, 2 * s + pairs[-1])
                place = probs_place(s, ffn)[:, heads, :]
                inverse = free_view(inv_sum[:, s % 2, heads], [[1, 2 * len(pairs)], [0, P]])
                done(probs_ready, dve.tensor_tensor(place, place, inverse, ALU.mult), len(pairs))

            def maxima(a, s, ffn):
                wait(scores_done, dve, a, s)
                dve.memset(wait_taker[:, :], 0.0)
                mask = mask_start if (isinstance(a, int) and a == 0 and s < NG) else mask_tile
                for h in range(HG):
                    unit = bank32[score_bank(s, ffn)][:, h * P:(h + 1) * P]
                    last = dve.tensor_tensor_reduce(out=unit, in0=unit, in1=mask[:, :], scale=1.0, scalar=MASKED,
                                                    op0=ALU.add, op1=ALU.max, accum_out=row_max[:, s % 2, h:h + 1])
                done(max_done, last)

            def bias(a, s, ffn):
                wait(max_done, dve, a, s)
                done(bias_done, dve.tensor_scalar(neg_max[:, s % 2, :], row_max[:, s % 2, :],
                                                   qk_scale[:, int(ffn), 3:4], None, ALU.mult))

            def swiglu(f, s):
                tmp = ffn_tmp[:, s % 2, :]
                wait(tanh_done, dve, f, s)
                done(gated, dve.scalar_tensor_tensor(out=tmp, in0=tmp, scalar=1.0, in1=bank32[2 * (s % 2)],
                                                      op0=ALU.add, op1=ALU.mult))
                wait(up_done, dve, f, s)
                wait(gated, dve, f, s)
                done(fused, dve.scalar_tensor_tensor(out=tmp, in0=bank32[2 * (s % 2) + 1],
                                                      scalar=fuse_scale[:, s:s + 1], in1=tmp,
                                                      op0=ALU.mult, op1=ALU.mult))

            def add_x(a, j, ffn):
                wait(proj_done, dve, a, j)
                done(proj_read, dve.tensor_tensor(x1[:, j, :], bank32[proj_bank(j, ffn)], x_rows[:, j, :], ALU.add))

            def moments(chain, tile, first, rows, z):
                st, mv = stats[:, z, :], mean_var[:, z, :]
                done(chain, dve.bn_stats(st, rows))
                wait(chain, dve, tile, first)
                dve.tensor_tensor(mv[:, 0:2], st[:, 1:3], st[:, 4:6], ALU.add)
                done(chain, dve.tensor_tensor(mv[:, 2:3], st[:, 1:2], st[:, 4:5], ALU.subtract))
                wait(chain, dve, tile, first + 1)
                dve.tensor_scalar(mv[:, 0:1], mv[:, 0:1], 0.5, None, ALU.mult)
                dve.scalar_tensor_tensor(out=mv[:, 3:4], in0=mv[:, 2:3], scalar=0.25, in1=mv[:, 2:3],
                                         op0=ALU.mult, op1=ALU.mult)
                done(chain, dve.tensor_scalar(mv[:, 1:2], mv[:, 1:2], 1.0 / EMB, EPS, ALU.mult, ALU.add))
                wait(chain, dve, tile, first + 2)
                done(chain, dve.tensor_tensor(mv[:, 1:2], mv[:, 1:2], mv[:, 3:4], ALU.add))

            def body(t, attn, ffn):
                a, f = t, t - 1
                if attn:
                    before = qkT[:, 2 * NB, :, WINDOW:P]
                    if ffn:
                        wait_qkT(dve, a - 1, NB - 1, NG - 1)
                        dve.wait_ge(setup, SETUP_ALL)
                        done(k_carried, dve.tensor_copy(before, qkT[:, NB, :, WINDOW:P]))
                    else:
                        done(k_carried, dve.memset(before, 0.0))
                    dve.wait_ge(tables_in, (a + 1) * 16)
                    flat = tables[:, :, :, :].rearrange("p b c i -> p (b c i)")
                    done(tables_scaled, dve.tensor_scalar(flat, flat, qk_scale[:, int(ffn), 1:2], None, ALU.mult))
                    wait(tables_scaled, dve, a, 0)
                    for j in range(NB):
                        if j:
                            keep_qkT(a, j - 1, 0)
                            keep_qkT(a, j - 1, 2)
                        if j < NB - 1:
                            rope_products(a, j)
                            rope_sums(a, j)
                            split_low(a, j)
                            if not ffn:
                                for i in range(sum(SEARCHED[:j]), sum(SEARCHED[:j + 1])):
                                    search(i)
                for s in range(STEPS):
                    if attn and (ffn or s == 0):
                        maxima(a, s, ffn)
                        bias(a, s, ffn)
                    ahead = attn and not ffn and s + 1 < STEPS
                    if ahead:
                        maxima(a, s + 1, ffn)
                    if ffn and s:
                        swiglu(f, s - 1)
                    if attn:
                        if s == 0:
                            rope_products(a, NB - 1, (0, 3))
                        for pairs in (range(0, 1), range(1, 2)) if ffn else (range(2),):
                            invert_sums(a, s, pairs)
                            if ahead:
                                bias(a, s + 1, ffn)
                            weights(a, s, ffn, pairs)
                        if s == 0:
                            rope_products(a, NB - 1, (1, 2))
                        if s == 1:
                            rope_sums(a, NB - 1)
                        if 0 <= s - SPLIT_FROM < 4:
                            split_low(a, NB - 1, [s - SPLIT_FROM])
                        if 0 <= s - TURN_AT - int(not ffn) < NG:
                            keep_qkT(a, NB - 1, s - TURN_AT - int(not ffn))
                        if not ffn and s >= SEARCH_FROM:
                            search(sum(SEARCHED) + s - SEARCH_FROM)
                if attn and not ffn:
                    for i in range(AT_END, HALVES):
                        search(i)
                    dve.wait_ge(halves_searched, HALVES)
                    dve.tensor_reduce(largest[:, 3:4], half_max[:, :], AX.X, ALU.max).then_inc(halves_searched, 1)
                    setup_others()
                if ffn:
                    swiglu(f, STEPS - 1)
                for j in range(NB):
                    rows_y, rows_x1 = y[:, j % 2, :], x1[:, j, :]
                    if ffn:
                        wait(down_done, dve, f, j)
                        dve.wait_ge(y_moved[j % 2], (f * (NB // 2) + (j // 2 + 1)) * 16)
                        done(down_read, dve.tensor_tensor(rows_y, bank32[j % 2], sdown[:, :], ALU.mult))
                        wait(down_read, dve, f, j)
                        done(ln2_chain, dve.tensor_tensor(rows_y, rows_y, rows_x1, ALU.add))
                        wait(ln2_chain, dve, f, 5 * j)
                        moments(ln2_chain, f, 5 * j + 1, rows_y, 1)
                    if attn:
                        if j == 0:
                            dve.wait_ge(rows_in, (a + 1) * 16)
                        if ffn:
                            add_x(a, j, ffn)
                        else:
                            for block in ((0,), (1,), (2, 3), ())[j]:
                                add_x(a, block, ffn)
                        wait(proj_read, dve, a, j)
                        moments(ln1_chain, a, 4 * j, rows_x1, 0)
                    if ffn:
                        wait(rstd2, dve, f, j)
                        done(y_ready, dve.tensor_scalar(rows_y, rows_y, mean_var[:, 1, 0:1], rstd[:, 1:2],
                                                         ALU.subtract, ALU.mult))
                    if attn:
                        wait(rstd1, dve, a, j)
                        done(x1_ready, dve.tensor_scalar(rows_x1, rows_x1, mean_var[:, 0, 0:1], rstd[:, 0:1],
                                                          ALU.subtract, ALU.mult))
                        wait(x1_high, dve, a, j)
                        done(x1_low, dve.scalar_tensor_tensor(out=x1_split[:, j, 1, :], in0=rows_x1, scalar=X1_SCALE,
                                                               in1=x1_split[:, j, 0, :], op0=ALU.mult,
                                                               op1=ALU.subtract))

            count = [4]

            def chained(instruction):
                count[0] += 1
                instruction.then_inc(setup, 1)
                dve.wait_ge(setup, count[0])

            def to_powers(big):
                chained(dve.tensor_scalar(big, big, 1e-12, None, ALU.max))
                chained(dve.tensor_scalar(big.bitcast(I32), big.bitcast(I32), EXPONENT_BITS, None, ALU.bitwise_and))

            def scores_scales(z):
                place = [qk_scale[:, z, i:i + 1] for i in range(4)]
                chained(dve.tensor_tensor(place[0], power[:, 3 * z:3 * z + 1], power[:, 1:2], ALU.mult))
                chained(dve.tensor_scalar(place[0], place[0], 0.125, None, ALU.mult))
                chained(dve.reciprocal(place[1], place[0]))
                chained(dve.tensor_scalar(place[2], place[0], place[0], SCALE, ALU.mult, ALU.mult))
                chained(dve.tensor_scalar(place[3], place[2], -1.0, None, ALU.mult))

            def setup_others():
                dve.wait_ge(pool_setup, 3)
                to_powers(power[:, 3:4])
                scores_scales(1)
                chained(dve.tensor_scalar(carry_scale[:, :], qk_scale[:, 0, 0:1], qk_scale[:, 1, 1:2], None, ALU.mult))
                wait_qkT(dve, 0, NB - 1, NG - 1)
                wait(pv_done, dve, 0, STEPS - 1)
                last_k = qkT[:, NB, :, WINDOW:P]
                chained(dve.tensor_scalar(last_k, last_k, carry_scale[:, :], None, ALU.mult))
                chained(dve.reciprocal(fuse_inv[:, :], power[:, 2:3]))
                chained(dve.tensor_scalar(fuse_scale[:, :], fuse_scale[:, :], fuse_inv[:, :],
                                          0.5 * 2.0 ** -18 / X1_SCALE ** 2, ALU.mult, ALU.mult))
                dve.wait_ge(sdown_in, 16)
                chained(dve.tensor_scalar(sdown[:, :], sdown[:, :], power[:, 2:3], 2.0 ** 18, ALU.mult, ALU.mult))
                assert count[0] == SETUP_ALL

            dve.memset(v_cross[WINDOW:P, 0, :], 0.0)
            dve.wait_ge(const_in, 3 * 16)
            for i in range(2):
                dve.wait_ge(y_moved[i], 16)
            dve.tensor_copy(eye32[:, :], raw_const[:, 0:P])
            dve.tensor_copy(eye16[:, :], raw_const[:, 0:P])
            dve.tensor_copy(mask_tile[:, :], raw_const[:, P:2 * P])
            dve.tensor_copy(mask_start[:, :], raw_const[:, 2 * P:3 * P])
            dve.tensor_scalar(tanh_scale[:, :], s_raw[:, 0:STEPS], 0.5 / X1_SCALE, None, ALU.mult)
            dve.tensor_tensor(fuse_scale[:, :], s_raw[:, 0:STEPS], s_raw[:, STEPS:2 * STEPS], ALU.mult)\
                .then_inc(consts_ready, 1)
            dve.wait_ge(consts_ready, 1)
            dve.tensor_reduce(largest[:, 2:3], fuse_scale[:, :], AX.X, ALU.max,
                              apply_absolute_value=True).then_inc(setup, 1)
            for part in range(2):
                if part == 1:
                    dve.wait_ge(rows_in, 16)
                    dve.tensor_reduce(half_max[:, 0:1], x_rows, AX.XY, ALU.max, apply_absolute_value=True)\
                        .then_inc(setup, 1)
                dve.wait_ge(wqkv_in[part], 16)
                dve.tensor_reduce(part_max[:, part:part + 1], wqkv[:, :, part * EMB:(part + 1) * EMB], AX.XY, ALU.max,
                                  apply_absolute_value=True).then_inc(setup, 1)
            dve.wait_ge(setup, 4)
            dve.tensor_copy(largest[:, 0:1], half_max[:, 0:1])
            chained(dve.tensor_tensor(largest[:, 1:2], part_max[:, 0:1], part_max[:, 1:2], ALU.max))
            dve.wait_ge(pool_setup, 2)
            to_powers(power[:, 0:3])
            scores_scales(0)
            bodies(dve, body)


_OUT = (1, 4096, 512)


def kernel(L0_attn_x, L0_attn_w_qkv, L0_attn_w_out, L0_attn_w_c1, L0_attn_w_c2, L0_ffn_w_gate, L0_ffn_w_up,
           L0_ffn_w_down, L0_ffn_s_gate, L0_ffn_s_up, L0_ffn_s_down):
    import numpy as np
    import concourse.bacc as bacc
    from concourse.bass_utils import run_bass_kernel_spmd

    x = np.asarray(L0_attn_x)[0]
    n_rows = x.shape[0]
    w = np.asarray(L0_attn_w_qkv)
    q, k, v = w[0:EMB], w[EMB:2 * EMB], w[2 * EMB:3 * EMB]
    w_qkvT = np.ascontiguousarray(np.concatenate([q[0::2], k[0::2], q[1::2], k[1::2], v], axis=0).T)

    inv_freq = np.float32(1.0) / np.power(np.float32(10000.0),
                                          np.arange(0, HEAD_DIM, 2, dtype=np.float32) / np.float32(HEAD_DIM))
    freqs = np.outer(np.arange(n_rows, dtype=np.float32), inv_freq.astype(np.float32))
    cos, sin = np.cos(freqs), np.sin(freqs)
    even = np.arange(0, HEAD_DIM, 2) % HALF
    odd = np.arange(1, HEAD_DIM, 2) % HALF
    rope = np.concatenate([cos[:, even], sin[:, even], cos[:, odd], sin[:, odd]], axis=1).astype(np.float32)

    row, key = np.arange(WINDOW)[:, None], np.arange(WINDOW)[None, :]
    own = np.where(key <= row, 0.0, MASKED)
    earlier = np.where(key > row, 0.0, MASKED)
    nothing = np.full((WINDOW, WINDOW), MASKED)
    mask_mid = np.block([[own, earlier], [earlier, own]]).astype(np.float32)
    mask_first = np.block([[own, nothing], [earlier, own]]).astype(np.float32)

    arrays = {
        "x": x,
        "xT": np.ascontiguousarray(x.T),
        "w_qkvT": w_qkvT,
        "w_outT": np.ascontiguousarray(np.asarray(L0_attn_w_out).T),
        "w_gate": np.ascontiguousarray(L0_ffn_w_gate).view(np.int32),
        "w_up": np.ascontiguousarray(L0_ffn_w_up).view(np.int32),
        "w_down": np.ascontiguousarray(L0_ffn_w_down).view(np.int32),
        "s_gate": np.ascontiguousarray(np.asarray(L0_ffn_s_gate).reshape(STEPS, P).T),
        "s_up": np.ascontiguousarray(np.asarray(L0_ffn_s_up).reshape(STEPS, P).T),
        "s_down": np.ascontiguousarray(np.asarray(L0_ffn_s_down).reshape(1, EMB)),
        "rope": rope,
        "mask_mid": mask_mid,
        "mask_first": mask_first,
        "eye": np.eye(P, dtype=np.float32),
    }
    nc = bacc.Bacc("TRN2", target_bir_lowering=False, num_devices=1)
    args = [nc.dram_tensor(n, a.shape, mybir.dt.from_np(a.dtype), kind="ExternalInput").ap()
            for n, a in arrays.items()]
    out = nc.dram_tensor("out", (n_rows, EMB), F32, kind="ExternalOutput").ap()
    build(nc, *args, out)
    result = run_bass_kernel_spmd(nc, [arrays], core_ids=[0])
    return result.results[0]["out"].reshape(_OUT)
```
